# Optimizing a Trainium2 kernel written in Bass

```python
import numpy as np
import jax
import jax.numpy as jnp

def _softmax(x, axis=-1):
    return jax.nn.softmax(x, axis=axis)

def _gelu(x):
    return jax.nn.gelu(x, approximate=True)

def _silu(x):
    return jax.nn.silu(x)

def _sigmoid(x):
    return jax.nn.sigmoid(x)

def _layernorm(x, axis=-1, eps=1e-05):
    m = jnp.mean(x, axis=axis, keepdims=True)
    v = jnp.var(x, axis=axis, keepdims=True)
    return (x - m) / jnp.sqrt(v + eps)

def _scatter_add(tgt, idx, src, axis=0):
    return tgt.at[idx].add(src)

def _segment_sum(src, seg, n):
    return jax.ops.segment_sum(src, seg, n)
kernel_name = 'mk_macaron_d1_jaxref_r4_257eb4'

def setup_inputs(seed: int=0):
    np.random.seed(seed)
    _w = jnp.asarray

    def _L0_attn_setup():
        import jax, jax.numpy as jnp
        import numpy as np
        MASK_VAL = -1000000000.0
        D_MODEL = 256
        N_HEADS = 16
        key = jax.random.key(seed)
        ks = jax.random.split(key, 7)
        b, n, d = (2, 512, D_MODEL)

        def xavier(k, shape):
            fan_in, fan_out = (shape[1], shape[0])
            lim = float(np.sqrt(6.0 / (fan_in + fan_out)))
            return jax.random.uniform(k, shape, jnp.float32, -lim, lim)
        return {'x': jax.random.normal(ks[0], (b, n, d), jnp.float32), 'Wq': xavier(ks[1], (d, d)), 'bq': jnp.zeros((d,), jnp.float32), 'Wkv': xavier(ks[2], (2 * d, d)), 'bkv': jnp.zeros((2 * d,), jnp.float32), 'Wo': xavier(ks[3], (d, d)), 'bo': jnp.zeros((d,), jnp.float32)}
    _L0_attn_in = _L0_attn_setup()

    def _L0_ffn_setup():
        import jax, jax.numpy as jnp
        import numpy as np
        CAPACITY_FACTOR = 1.25
        key = jax.random.key(seed)
        ks = jax.random.split(key, 6)
        B, S, H, E = (4, 1024, 256, 8)
        scale = 1.0 / np.sqrt(H)
        return {'tokens': jax.random.normal(ks[0], (B, S, H), dtype=jnp.float32), 'gate_w': jax.random.normal(ks[1], (E, H), dtype=jnp.float32) * scale, 'w1': jax.random.normal(ks[2], (E, H, H), dtype=jnp.float32) * scale, 'b1': jax.random.normal(ks[3], (E, H), dtype=jnp.float32) * 0.01, 'w2': jax.random.normal(ks[4], (E, H, H), dtype=jnp.float32) * scale, 'b2': jax.random.normal(ks[5], (E, H), dtype=jnp.float32) * 0.01}
    _L0_ffn_in = _L0_ffn_setup()
    _d = {'L0_attn_x': _L0_attn_in['x'], 'L0_attn_Wq': _L0_attn_in['Wq'], 'L0_attn_bq': _L0_attn_in['bq'], 'L0_attn_Wkv': _L0_attn_in['Wkv'], 'L0_attn_bkv': _L0_attn_in['bkv'], 'L0_attn_Wo': _L0_attn_in['Wo'], 'L0_attn_bo': _L0_attn_in['bo'], 'L0_ffn_gate_w': _L0_ffn_in['gate_w'], 'L0_ffn_w1': _L0_ffn_in['w1'], 'L0_ffn_b1': _L0_ffn_in['b1'], 'L0_ffn_w2': _L0_ffn_in['w2'], 'L0_ffn_b2': _L0_ffn_in['b2']}
    _x0 = _d['L0_attn_x']
    _d['L0_attn_x'] = jax.random.normal(jax.random.fold_in(jax.random.key(seed), 1), (8, 1024, 256), dtype=_x0.dtype)
    del _x0
    return _d

def reference(L0_attn_x, L0_attn_Wq, L0_attn_bq, L0_attn_Wkv, L0_attn_bkv, L0_attn_Wo, L0_attn_bo, L0_ffn_gate_w, L0_ffn_w1, L0_ffn_b1, L0_ffn_w2, L0_ffn_b2):

    def _L0_attn_ref(x, Wq, bq, Wkv, bkv, Wo, bo):
        import jax, jax.numpy as jnp
        import numpy as np
        MASK_VAL = -1000000000.0
        D_MODEL = 256
        N_HEADS = 16
        b, n, d = x.shape
        h = N_HEADS
        hd = d // h
        scale = hd ** (-0.5)
        q = x @ Wq.T + bq
        kv = x @ Wkv.T + bkv
        k, v = jnp.split(kv, 2, axis=-1)

        def to_heads(t):
            return t.reshape(b, n, h, hd).transpose(0, 2, 1, 3)
        q, k, v = (to_heads(q), to_heads(k), to_heads(v))
        dots = jnp.einsum('bhid,bhjd->bhij', q * scale, k)
        causal = jnp.triu(jnp.ones((n, n), bool), k=1)
        dots = jnp.where(causal, MASK_VAL, dots)
        attn = jax.nn.softmax(dots, axis=-1)
        out = jnp.einsum('bhij,bhjd->bhid', attn, v)
        out = out.transpose(0, 2, 1, 3).reshape(b, n, d)
        return out @ Wo.T + bo

    def _L0_ffn_ref(tokens, gate_w, w1, b1, w2, b2):
        import jax, jax.numpy as jnp
        import numpy as np
        CAPACITY_FACTOR = 1.25
        B, S, H = tokens.shape
        E = gate_w.shape[0]
        N = B * S
        cap = int(CAPACITY_FACTOR * N / E)
        x = tokens.reshape(N, H)
        probs = jax.nn.softmax(x @ gate_w.T, axis=-1)
        top2_w, top2_idx = jax.lax.top_k(probs, 2)
        a_e = top2_idx.reshape(-1)
        a_w = top2_w.reshape(-1)
        tok_id = jnp.arange(2 * N) // 2
        counts = jnp.bincount(a_e, length=E)
        keep = counts <= cap
        valid = keep[a_e]
        onehot = jax.nn.one_hot(a_e, E, dtype=jnp.int32)
        pos = jnp.take_along_axis(jnp.cumsum(onehot, axis=0) - 1, a_e[:, None], axis=1)[:, 0]
        p = jnp.where(valid, jnp.minimum(pos, cap - 1), cap)
        x_a = x[tok_id]
        buf = jnp.zeros((E, cap + 1, H), dtype=x.dtype).at[a_e, p].set(x_a)
        h = jax.nn.silu(jnp.einsum('ech,efh->ecf', buf, w1) + b1[:, None, :])
        y = jnp.einsum('ecf,egf->ecg', h, w2) + b2[:, None, :]
        contrib = y[a_e, p] * (a_w * valid.astype(x.dtype))[:, None]
        out = contrib.reshape(N, 2, H).sum(axis=1)
        return out.reshape(B, S, H)
    x = L0_attn_x
    x = x + 0.5 * _L0_ffn_ref(_layernorm(x, axis=-1), L0_ffn_gate_w, L0_ffn_w1, L0_ffn_b1, L0_ffn_w2, L0_ffn_b2)
    x = x + _L0_attn_ref(_layernorm(x, axis=-1), L0_attn_Wq, L0_attn_bq, L0_attn_Wkv, L0_attn_bkv, L0_attn_Wo, L0_attn_bo)
    x = x + 0.5 * _L0_ffn_ref(_layernorm(x, axis=-1), L0_ffn_gate_w, L0_ffn_w1, L0_ffn_b1, L0_ffn_w2, L0_ffn_b2)
    return x

_drawn_inputs = setup_inputs


def setup_inputs(seed=0):
    import zlib

    import numpy as np

    out = dict(_drawn_inputs(seed))
    spreads = {'L0_attn_bq': (0.0, 0.8), 'L0_attn_bkv': (0.0, 0.1), 'L0_attn_bo': (0.0, 0.1)}
    factors = {}
    for name, (base, spread) in spreads.items():
        noise = np.random.default_rng([zlib.crc32(name.encode()), seed]).standard_normal(out[name].shape)
        drawn = base * np.exp(spread * noise) if base else spread * noise
        out[name] = jnp.asarray(drawn.astype(out[name].dtype))
    for name, factor in factors.items():
        out[name] = (out[name] * factor).astype(out[name].dtype)
    return out
```

```python
import concourse.bass as bass
from concourse import mybir
from contextlib import ExitStack

FP32 = mybir.dt.float32
BF16 = mybir.dt.bfloat16
INT32 = mybir.dt.int32
ALU = mybir.AluOpType
ACT = mybir.ActivationFunctionType
AX = mybir.AxisListType
ADD_REDUCE = bass.bass_isa.ReduceOp.add

B, S, D = 8, 1024, 256
H, HD = 16, 16
HG, NG = 4, 4
P = 128
TB = S // P
NT = B * TB
DC = D // P
CW = 512
CT = CW // P
NCH = B * S // CW
E = 8
CAP = int(1.25 * B * S / E)
EPS = 1e-5
KROWS = 6 * HD
MROWS = 3
VW = HD + 1
BIG = 3.0e38
NU = 48
NGRP = NU // HG
RUNS = ((0, 3, 0), (3, 2, 1), (5, 1, 2))
STACK_DMAS = 2 * len(RUNS)


MAX_GROUPS = 8


def group_shape(g):
    if g < CT:
        return 0, g, g * P, True
    jb = g - CT
    return 1, jb, max(0, jb - CT) * P, jb >= CT


def max_units():
    full = [(ib, h, 0, CW, False) for ib in range(CT, TB) for h in range(HG)]
    diag = [(ib, h, ib // CT * CW, (ib % CT + 1) * P, True) for ib in range(TB) for h in range(HG)]
    out = []
    for i, f in enumerate(full):
        out += [f, diag[2 * i], diag[2 * i + 1]]
    return out


MAX_UNITS = max_units()


def step_plan(hg, prev, nxt):
    extra = {}

    def put(g, pos, *events):
        extra.setdefault((g, pos), []).extend(events)

    def norm_jobs(kind, c, g):
        for t in range(CT):
            put(g, t, ("lnstat", kind, c, t))
            put(g + 2, t, ("lnnorm", kind, c, t))
        put(g + 1, 0, ("lnaggr", kind, c))

    def project(hq, g):
        for c in range(2):
            put(g + 2 * c, 1, ("use", "qk", hq, c))
            put(g + 2 * c, 3, ("q2", hq, c))
            put(g + 2 * c + 1, 1, ("q3", hq, c))

    if hg == 0:
        for j in range(4):
            put(1, min(j + 1, 3), ("use", "v", j))
        if prev:
            put(2, 0, ("use", "otr", 3, 0))
            put(2, 2, ("use", "otr", 3, 1))
        project(3, 3)
        if nxt:
            norm_jobs("x", 0, 3)
            put(6, 1, ("use", "xt", 0, 0))
            put(6, 3, ("use", "xt", 0, 1))
            norm_jobs("x", 1, 7)
            put(10, 1, ("use", "xt", 1, 0))
            put(10, 3, ("use", "xt", 1, 1))
    if hg == 1:
        put(2, 0, ("bo", 0))
        put(5, 0, ("bo", 1))
        put(7, 0, ("bo", 2))
        put(9, 0, ("bo", 3))
        if prev:
            for j in range(4):
                put(j, 0, ("use", "ont", j))
                put(j, 2, ("use", "wo", j))
            put(4, 0, ("out",))
        put(4, 1, ("use", "otr", 0, 0))
        put(4, 3, ("use", "otr", 0, 1))
        if nxt:
            project(0, 1)
    if hg == 2:
        put(1, 1, ("use", "otr", 1, 0))
        put(1, 3, ("use", "otr", 1, 1))
        if prev:
            for c in range(2):
                norm_jobs("g", c, 4 * c)
                put(4 * c + 3, 0, ("use", "xg", c, 0))
                put(4 * c + 3, 2, ("use", "xg", c, 1))
                put(4 * c + 4, 1, ("use", "lg", c))
                put(4 * c + 4, 3, ("use", "lt", c))
        if nxt:
            project(1, 2)
    if hg == 3:
        put(1, 1, ("use", "otr", 2, 0))
        put(1, 3, ("use", "otr", 2, 1))
        if nxt:
            project(2, 2)
    maxima = hg < NG - 1 or nxt
    if maxima:
        put(MAX_GROUPS, 0, ("mfin",))
        put(MAX_GROUPS + 1, 1, ("use", "mtr"))
        put(MAX_GROUPS + 1, 1, ("mdma",))
    plan, u = [], 0
    for g in range(NGRP):
        for h in range(HG):
            plan.append(("st", g, h))
            if h == 0 and not (hg == 0 and not prev and g < 2):
                plan.append(("pv", (g - 2) % NGRP))
                if g == 1:
                    plan.append(("oev", 1))
                if g == CT + 1:
                    plan.append(("oev", 0))
            if maxima:
                due = NU * (HG * g + h + 1) // (HG * MAX_GROUPS)
                while u < min(due, NU):
                    plan.append(("s", u))
                    u += 1
            plan += extra.get((g, h), [])
    return [(hg,) + e for e in plan]


def batch_plan(prev, nxt):
    return [e for hg in range(NG) for e in step_plan(hg, prev, nxt)]


def prologue_plan():
    plan = []
    for c in range(2):
        plan += [(3, "lnstat", "x", c, t) for t in range(CT)] + [(3, "lnaggr", "x", c)]
        plan += [(3, "lnnorm", "x", c, t) for t in range(CT)]
        plan += [(3, "use", "xt", c, j) for j in range(2)]
    for hq in range(3):
        for c in range(2):
            plan += [(3, "use", "qk", hq, c), (3, "q2", hq, c), (3, "q3", hq, c)]
        if hq == 0:
            plan += [(3, "s", u) for u in range(NU)]
            plan += [(3, "mfin",), (3, "use", "mtr"), (3, "mdma",)]
    return plan


def epilogue_plan():
    plan = [(0, "pv", NGRP - 2), (0, "pv", NGRP - 1), (0, "oev", 1)] + [(0, "use", "otr", 3, c) for c in range(2)]
    for j in range(4):
        plan += [(0, "use", "ont", j), (0, "use", "wo", j)]
    plan += [(0, "out")]
    for c in range(2):
        plan += [(0, "lnstat", "g", c, t) for t in range(CT)] + [(0, "lnaggr", "g", c)]
        plan += [(0, "lnnorm", "g", c, t) for t in range(CT)]
        plan += [(0, "use", "xg", c, j) for j in range(2)] + [(0, "use", "lg", c), (0, "use", "lt", c)]
    return plan


def count(plan, kind):
    return sum(e[1] == kind for e in plan)


def make_sections():
    before = {"use": 4 * NCH, "lnaggr": NCH, "lnnorm": CT * NCH}
    out = []
    for plan, times, b in ((prologue_plan(), 1, -1), (batch_plan(False, True), 1, 0),
                           (batch_plan(True, True), B - 2, 1), (batch_plan(True, False), 1, B - 1),
                           (epilogue_plan(), 1, B)):
        out.append((plan, times, b, dict(before)))
        for k in before:
            before[k] += times * count(plan, k)
    return out, before


SECTIONS, COUNTS_AFTER = make_sections()


def walk(eng, handle):
    for plan, times, b0, start in SECTIONS:
        def events(b):
            seen = dict.fromkeys(start, 0)
            for hg, kind, *a in plan:
                def n(k, more=0):
                    if times == 1:
                        return start[k] + seen[k] + more
                    per = count(plan, k)
                    return b * per + (start[k] + seen[k] + more - per * b0)
                handle(b, n, hg, kind, *a)
                if kind in seen:
                    seen[kind] += 1
        if times == 1:
            events(b0)
        else:
            with eng.Fori(b0, b0 + times) as b:
                events(b)


def wait(eng, sem, value):
    if not isinstance(value, int) or value > 0:
        eng.wait_ge(sem, value)


def program(nc, x, wqk_t, wv_t, wo_t, bqk, bv, bo, gate_t, w1_t, b1, w2_t, b2, out):
    with ExitStack() as ctx:
        ctx.enter_context(nc.allow_non_contiguous_dma(reason="biases and gate columns"))

        def sb(name, shape, dt=FP32):
            return ctx.enter_context(nc.sbuf_tensor(name, shape, dt))

        def pb(name):
            return ctx.enter_context(nc.psum_tensor(name, [P, CW], FP32))

        def sem(name):
            return ctx.enter_context(nc.semaphore(name))

        x_all = sb("x_all", [P, NT, D])
        w_qk = sb("w_qk", [P, DC, NG, P])
        w_v = sb("w_v", [P, DC, D])
        w_o = sb("w_o", [P, DC, D])
        w_gate = sb("w_gate", [P, DC, 32])
        qk_bias = sb("qk_bias", [P, NG])
        qk_scale = sb("qk_scale", [P, 1])
        v_bias = sb("v_bias", [P, DC])
        bo_row = sb("bo_row", [P, 1, D])
        ident = sb("ident", [P, P])
        ident16 = sb("ident16", [P, P], BF16)
        causal = sb("causal", [P, CW], BF16)
        neg_half = sb("neg_half", [P, CT])
        stats = sb("stats", [P, CT, 6])
        mean_var = sb("mean_var", [P, CT, 2])
        rstd = sb("rstd", [P, CT])
        xn = sb("xn", [P, CT, D])
        x_t = sb("x_t", [P, DC, S])
        xg_t = sb("xg_t", [P, DC, CW])
        qk32 = sb("qk32", [P, CW])
        rest = sb("rest", [P, CW])
        parts = sb("parts", [P, 2, 3, CW], BF16)
        q_stack = sb("q_stack", [P, NG, HG, S], BF16)
        k_stack = sb("k_stack", [P, NG, HG, S], BF16)
        v_aug = sb("v_aug", [P, TB, H, VW])
        probs = sb("probs", [P, 2, HG, CW])
        o_raw = sb("o_raw", [P, S])
        sum_inv = sb("sum_inv", [P, CT * HG, 1])
        o_tok = sb("o_tok", [P, TB, D])
        o_t = sb("o_t", [P, DC, 2 * P])
        max_diag = sb("max_diag", [P, HG, TB])
        max_full = sb("max_full", [P, HG, CT])
        max_rest = sb("max_rest", [P, HG, TB])
        max_parts = sb("max_parts", [P, MROWS, HG, TB], BF16)
        max_t = sb("max_t", [HG * MROWS * TB, P], BF16)
        lg_t = sb("lg_t", [P, P])
        logits = sb("logits", [P, NT, E])
        rank = sb("rank", [P, 1, E])
        top = sb("top", [P, NT, 1])
        best = sb("best", [P, NT, 1])
        counts = sb("counts", [P, E])
        total = sb("total", [P, E])
        kept = sb("kept", [P, 1, E])
        any_kept = sb("any_kept", [P, 1])
        flag = sb("flag", [P, 1], INT32)
        chosen, work, left = (probs[:, 0, i, :].rearrange("p (t e) -> p t e", e=E) for i in range(3))
        moe_space = q_stack[:, :, :, :].rearrange("p g h s -> p (g h s)").bitcast(FP32)
        w1_e = moe_space[:, 0:512].rearrange("p (c f) -> p c f", c=DC)
        w2_e = moe_space[:, 512:1024].rearrange("p (c f) -> p c f", c=DC)
        b2_e = moe_space[:, 1024:1280].rearrange("p (t f) -> p t f", t=1)
        b1_e = moe_space[:, 1280:1282]
        hidden = moe_space[:, 2048:3072].rearrange("p (c t) -> p c t", c=DC)
        hidden_e = moe_space[:, 3072:4096].rearrange("p (c t) -> p c t", c=DC)
        y_e = moe_space[:, 4096:5120].rearrange("p (t f) -> p t f", t=CT)

        st_bank = [pb(f"st{i}") for i in range(3)]
        s_bank = [pb(f"s{i}") for i in range(3)]
        o_bank = pb("o_bank")
        misc = pb("misc")
        misc16 = misc[:, :].bitcast(BF16)

        part_dram = nc.dram_tensor("part_dram", [NG, 2, 3, HG * HD, S], BF16, kind="Internal").ap()

        weights_in = sem("weights_in")
        consts_ready = sem("consts_ready")
        consts_step = sem("consts_step")
        x_in = [sem(f"x_in{i}") for i in range(4)]
        misc_full = sem("misc_full")
        misc_free = sem("misc_free")
        stats_ready = sem("stats_ready")
        rstd_ready = sem("rstd_ready")
        xn_ready = sem("xn_ready")
        rest_ready = sem("rest_ready")
        part2_ready = sem("part2_ready")
        part3_ready = sem("part3_ready")
        parts_out = [sem(f"parts_out{i}") for i in range(2)]
        stack_in = [sem(f"stack_in{i}") for i in range(NG)]
        st_full = sem("st_full")
        exp_done = sem("exp_done")
        sel_done = sem("sel_done")
        pv_done = sem("pv_done")
        o_out = sem("o_out")
        s_full = sem("s_full")
        max_done = sem("max_done")
        mparts_ready = sem("mparts_ready")
        max_in = [sem(f"max_in{i}") for i in range(NG)]
        bo_added = sem("bo_added")
        out_written = sem("out_written")
        counted = sem("counted")
        totalled = sem("totalled")
        flag_ready = sem("flag_ready")
        baton = [sem(f"baton{i}") for i in range(2)]
        moe_weights_in = [sem(f"moe_weights_in{i}") for i in range(2)]

        wait_passed = {name: sem(f"wait_passed_{name}") for name in ("sync", "gpsimd", "vector")}

        WEIGHT_DMAS = 7
        CONSTS = 2
        MIDDLE = B - 2
        STACK_IN, MAX_IN = 16 * STACK_DMAS, 16
        GATE_TURNS, CHUNK_TURNS, EXPERT_TURNS = 3, 5, 5
        TURNS = CHUNK_TURNS + E * EXPERT_TURNS

        def lin(b, k, c):
            return b * k + c

        def passed(eng, name):
            eng.sem_inc(wait_passed[name], 1)

        def x_tiles(t0, n):
            return x_all[:, bass.ds(t0, n), :]

        def row_out(t, width):
            return misc[:, t * width:(t + 1) * width]

        def vector_stats(t, tile):
            nc.vector.bn_stats(stats[:, t, :], x_tiles(tile, 1)[:, 0, :])

        def vector_aggregate(eng):
            eng.drain()
            for t in range(CT):
                last = nc.vector.bn_aggr(mean_var[:, t, :], stats[:, t, :])
            return last

        def vector_normalise(t, tile):
            return nc.vector.tensor_scalar(xn[:, t, :], x_tiles(tile, 1)[:, 0, :], mean_var[:, t, 0:1],
                                           rstd[:, t:t + 1], ALU.subtract, ALU.mult)

        def pool_rstd(eng, fenced, value):
            nc.gpsimd.tensor_scalar_add(rstd[:, :], mean_var[:, :, 1], EPS).then_inc(fenced, 1)
            eng.wait_ge(fenced, value)
            return nc.gpsimd.tensor_tensor(rstd[:, :], rstd[:, :], neg_half[:, :], ALU.pow)

        rstd_sum = sem("rstd_sum")
        moe_rstd_sum = [sem(f"moe_rstd_sum{i}") for i in range(2)]

        def tensor_gate_logits():
            for dc in range(DC):
                for t in range(CT):
                    last = nc.tensor.matmul(misc[32 * t:32 * t + 32, 0:P], w_gate[:, dc, :],
                                            xg_t[:, dc, t * P:(t + 1) * P], start=dc == 0, stop=dc == DC - 1)
            return last

        def tensor_transpose_tiles(dst, src, t0):
            for dc in range(DC):
                for t in range(2):
                    i = 2 * dc + t
                    last = nc.tensor.transpose(dst[:, i * P:(i + 1) * P],
                                               src[:, t0 + t, dc * P:(dc + 1) * P], ident[:, :])
            return last

        def pair_view():
            return misc[:, :].rearrange("p (c t) -> p c t", c=DC)

        def logits_view():
            return misc[:, 0:P].rearrange("p (t e) -> p t e", t=CT)[:, :, 0:E]

        def moe_value(c, e, turn):
            if e is None:
                return c * TURNS + (GATE_TURNS + turn)
            return c * TURNS + (e * EXPERT_TURNS + (GATE_TURNS + CHUNK_TURNS + turn))

        def moe_experts(eng, layer, gate, chunk, expert):
            eng.wait_ge(flag_ready, layer + 1)
            kept_here = eng.value_load(flag[0:1, 0:1], min_val=0, max_val=1)
            with eng.If(kept_here > 0):
                if gate:
                    gate()
                with eng.Fori(0, NCH) as c:
                    if chunk:
                        chunk(c)
                    with eng.Fori(0, E) as e:
                        expert(c, e)
                eng.wait_ge(baton[layer], GATE_TURNS + NCH * TURNS)
            with eng.Else():
                eng.nop()

        block = ctx.enter_context(nc.Block())

        @block.sync
        def _(eng):
            for k in range(4):
                eng.dma_start(x_tiles(k * CT, CT), x[k * CT:(k + 1) * CT, :, :].rearrange("t p d -> p t d"))\
                   .then_inc(x_in[k], 16)
            with eng.Fori(1, NCH // 4) as i:
                for k in range(4):
                    eng.wait_ge(x_in[k], i * 16)
                    passed(eng, "sync")
                    eng.dma_start(x_tiles(i * (4 * CT) + k * CT, CT),
                                  x[bass.ds(i * (4 * CT) + k * CT, CT), :, :].rearrange("t p d -> p t d"))\
                       .then_inc(x_in[k], 16)

            def moe_sync(layer):
                def expert(c, e):
                    eng.wait_ge(baton[layer], moe_value(c, e, 0))
                    passed(eng, "sync")
                    for dst, src in ((w1_e, w1_t[bass.ds(e, 1), :, :].rearrange("e (c p) f -> p (e c) f", p=P)),
                                     (w2_e, w2_t[bass.ds(e, 1), :, :].rearrange("e (c p) f -> p (e c) f", p=P)),
                                     (b1_e, b1[bass.ds(e, 1), :].rearrange("e (c p) -> p (e c)", p=P)),
                                     (b2_e, b2[bass.ds(e, 1), :].partition_broadcast(P))):
                        eng.dma_start(dst, src).then_inc(moe_weights_in[layer], 16)
                moe_experts(eng, layer, None, None, expert)

            def handle(b, n, hg, kind, *a):
                if kind == "q3":
                    hq, c = a
                    m = (4, hq if hg == 0 else hq + NG)
                    eng.wait_ge(part3_ready, lin(b, 2 * m[0], 2 * m[1] + c + 1))
                    passed(eng, "sync")
                    if c == 0:
                        wait(eng, stack_in[hq], lin(b, STACK_IN, 0 if hg == 0 else STACK_IN))
                    for qk in range(2):
                        eng.dma_start(part_dram[hq, qk, :, :, c * CW:(c + 1) * CW].rearrange("k p c -> p k c"),
                                      parts[qk * HG * HD:(qk + 1) * HG * HD, c, :, :]).then_inc(parts_out[c], 16)
                    if c == 1:
                        for half in range(2):
                            eng.wait_ge(parts_out[half], lin(b, 32 * m[0], 32 * m[1] + 32))
                            passed(eng, "sync")
                        wait(eng, pv_done, lin(b, NGRP * m[0], NGRP * (m[1] - 3)))
                        for r, times, part in RUNS:
                            rows = slice(r * HD, (r + times) * HD)
                            eng.dma_start(q_stack[rows, hq, :, :].rearrange("r h c -> r (h c)"),
                                          part_dram[hq, 0, 0:times, :, :].rearrange("k (d h) c -> (k d) (h c)", h=HG))\
                               .then_inc(stack_in[hq], 16)
                            eng.dma_start(k_stack[rows, hq, :, :].rearrange("r h c -> r (h c)"),
                                          part_dram[hq, 1, part, :, :].rearrange("(d h) c -> d (h c)", h=HG)
                                          .partition_broadcast(times)).then_inc(stack_in[hq], 16)
                elif kind == "mdma":
                    hm = (hg + 1) % NG
                    eng.wait_ge(misc_free, n("use", 1))
                    eng.dma_start(q_stack[KROWS:KROWS + MROWS, hm, :, :].rearrange("k h (t c) -> k (h t) c", c=P),
                                  max_t[:, :]).then_inc(max_in[hm], 16)
                elif kind == "out":
                    eng.wait_ge(misc_free, n("use", 1))
                    passed(eng, "sync")
                    eng.dma_start(out[bass.ds(b * TB - TB, TB), :, :].rearrange("t p d -> p t d"),
                                  x_tiles(b * TB - TB, TB)).then_inc(out_written, 16)

            moe_sync(0)
            walk(eng, handle)
            eng.wait_ge(out_written, 16 * B)
            moe_sync(1)
            with eng.If(eng.value_load(flag[0:1, 0:1], min_val=0, max_val=1) > 0):
                eng.dma_start(out.rearrange("t p d -> p t d"), x_all[:, :, :]).then_inc(out_written, 16)
                eng.wait_ge(out_written, 16 * B + 16)
            with eng.Else():
                eng.nop()

        @block.gpsimd
        def _(eng):
            nc.gpsimd.memset(ident[:, :], 0.0)
            nc.gpsimd.memset(causal[:, :], 0.0)
            nc.gpsimd.memset(w_gate[:, :, E:32], 0.0)
            nc.gpsimd.memset(neg_half[:, :], -0.5)
            nc.gpsimd.memset(qk_scale[:, :], 1.0).then_inc(consts_step, 1)
            eng.wait_ge(consts_step, 1)
            nc.gpsimd.affine_select(out=ident[:, :], in_=ident[:, :], compare_op=ALU.not_equal, fill=1.0,
                                    base=0, pattern=[[-1, P]], channel_multiplier=1)
            nc.gpsimd.affine_select(out=causal[:, CW - P:CW], in_=causal[:, CW - P:CW], compare_op=ALU.is_ge,
                                    fill=-BIG, base=0, pattern=[[-1, P]], channel_multiplier=1)
            nc.gpsimd.memset(qk_scale[0:HG * HD, :], HD ** -0.5)
            for e in range(E):
                nc.gpsimd.memset(rank[:, 0, e:e + 1], float(E - e))
            nc.gpsimd.memset(v_aug[:, :, :, HD:VW], 1.0).then_inc(consts_step, 1)
            eng.wait_ge(consts_step, 2)
            nc.gpsimd.tensor_copy(ident16[:, :], ident[:, :]).then_inc(consts_ready, 1)

            with eng.Fori(0, NCH) as c:
                eng.wait_ge(stats_ready, c + 1)
                passed(eng, "gpsimd")
                pool_rstd(eng, rstd_sum, c + 1).then_inc(rstd_ready, 1)

            def moe_pool(layer):
                eng.wait_ge(counted, layer + 1)
                nc.gpsimd.partition_all_reduce(total[:, :], counts[:, :], P, ADD_REDUCE).then_inc(totalled, 1)

                def chunk(c):
                    eng.wait_ge(baton[layer], moe_value(c, None, 1))
                    passed(eng, "gpsimd")
                    pool_rstd(eng, moe_rstd_sum[layer], c + 1).then_inc(baton[layer], 1)

                moe_experts(eng, layer, None, chunk, lambda c, e: eng.nop())

            def handle(b, n, hg, kind, *a):
                if kind == "st":
                    g, h = a
                    if h == HG - 1 and group_shape(g)[3]:
                        eng.wait_ge(exp_done, lin(b, NU * NG, NU * hg + HG * g + HG))
                        passed(eng, "gpsimd")
                        now = probs[:, g % 2, :, 0:P]
                        nc.gpsimd.affine_select(out=now, in_=now, compare_op=ALU.is_ge, fill=0.0, base=0,
                                                pattern=[[0, HG], [1, P]], channel_multiplier=-1)\
                            .then_inc(sel_done, 1)
                elif kind == "lnaggr":
                    eng.wait_ge(stats_ready, n("lnaggr", 1))
                    passed(eng, "gpsimd")
                    pool_rstd(eng, rstd_sum, n("lnaggr", 1)).then_inc(rstd_ready, 1)
                elif kind == "use" and a[0] == "qk":
                    hq, c = a[1:]
                    m = hq if hg == 0 else hq + NG
                    wait(eng, part3_ready, lin(b, 2 * NG, 2 * m + c))
                    eng.wait_ge(misc_free, n("use", 2))
                    nc.gpsimd.tensor_tensor(rest[:, :], qk32[:, :], parts[:, c, 0, :], ALU.subtract)\
                        .then_inc(rest_ready, 1)
                elif kind == "q3":
                    hq, c = a
                    m = hq if hg == 0 else hq + NG
                    eng.wait_ge(part2_ready, lin(b, 2 * NG, 2 * m + c + 1))
                    nc.gpsimd.tensor_tensor(parts[:, c, 2, :], rest[:, :], parts[:, c, 1, :], ALU.subtract)\
                        .then_inc(part3_ready, 1)
                elif kind == "bo":
                    eng.wait_ge(xn_ready, n("lnnorm"))
                    now = x_tiles(b * TB + 2 * a[0], 2)
                    nc.gpsimd.tensor_tensor(now, now, bo_row[:, :, :].to_broadcast([P, 2, D]), ALU.add)\
                        .then_inc(bo_added, 1)

            eng.wait_ge(weights_in, 16 * WEIGHT_DMAS)
            moe_pool(0)
            walk(eng, handle)
            moe_pool(1)

        @block.scalar
        def _(eng):
            for dst, src in ((w_gate[:, :, 0:E], gate_t.rearrange("(c p) e -> p c e", p=P)),
                             (w_qk[:, :, :, :], wqk_t.rearrange("(c p) g f -> p c g f", p=P)),
                             (w_v[:, :, :], wv_t.rearrange("(c p) f -> p c f", p=P)),
                             (w_o[:, :, :], wo_t.rearrange("(c p) f -> p c f", p=P)),
                             (qk_bias[:, :], bqk.rearrange("g p -> p g")),
                             (v_bias[:, :], bv.rearrange("(c p) -> p c", p=P)),
                             (bo_row[:, :, :], bo.rearrange("(t d) -> t d", t=1).partition_broadcast(P))):
                eng.dma_start(dst, src).then_inc(weights_in, 16)
            eng.wait_ge(consts_ready, CONSTS)

            def gate_evictions(first, tile):
                for j in range(2):
                    eng.wait_ge(misc_full, first + (j + 1))
                    nc.scalar.activation(xg_t[:, :, 2 * j * P:2 * (j + 1) * P], pair_view(), ACT.Copy)\
                        .then_inc(misc_free, 1)
                eng.wait_ge(misc_full, first + 3)
                nc.scalar.activation(lg_t[:, :], misc[:, 0:P], ACT.Copy).then_inc(misc_free, 1)
                eng.wait_ge(misc_full, first + 4)
                nc.scalar.activation(logits[:, bass.ds(tile, CT), :], logits_view(), ACT.Copy)\
                    .then_inc(misc_free, 1)

            with eng.Fori(0, NCH) as c:
                gate_evictions(c * 4, c * CT)

            def moe_scalar(layer):
                def gate():
                    eng.wait_ge(baton[layer], 1)
                    nc.scalar.activation(work, left, ACT.Exp).then_inc(baton[layer], 1)

                def chunk(c):
                    eng.wait_ge(baton[layer], moe_value(c, None, 4))
                    for dc in range(DC):
                        last = nc.scalar.activation(xg_t[:, dc, :], st_bank[dc][:, :], ACT.Copy)
                    last.then_inc(baton[layer], 1)

                def expert(c, e):
                    eng.wait_ge(baton[layer], moe_value(c, e, 1))
                    for fc in range(DC):
                        nc.scalar.activation(hidden[:, fc, :], st_bank[fc][:, :], ACT.Identity,
                                             bias=b1_e[:, fc:fc + 1])
                    eng.drain()
                    nc.scalar.activation(hidden_e, hidden, ACT.Exp, scale=-1.0).then_inc(baton[layer], 1)

                moe_experts(eng, layer, gate, chunk, expert)

            def evict(b, n, hg, what, *a):
                if what in ("otr", "wo"):
                    return
                eng.wait_ge(misc_full, n("use", 1))
                if what == "v":
                    j = a[0]
                    nc.scalar.activation(v_aug[:, 2 * j:2 * j + 2, :, 0:HD],
                                         misc[:, :].rearrange("p (t h d) -> p t h d", t=2, d=HD), ACT.Copy)\
                        .then_inc(misc_free, 1)
                elif what == "qk":
                    hq, c = a
                    m = hq if hg == 0 else hq + NG
                    wait(eng, parts_out[c], lin(b, 32 * NG, 32 * m))
                    wait(eng, rest_ready, lin(b, 2 * NG, 2 * m + c))
                    for dst in (qk32[:, :], parts[:, c, 0, :]):
                        last = nc.scalar.activation(dst, misc[:, :], ACT.Identity, bias=qk_bias[:, hq:hq + 1],
                                                    scale=qk_scale[:, :])
                    last.then_inc(misc_free, 1)
                elif what == "xt":
                    c, j = a
                    t0 = c * CW + 2 * j * P
                    nc.scalar.activation(x_t[:, :, t0:t0 + 2 * P], pair_view(), ACT.Copy).then_inc(misc_free, 1)
                elif what == "xg":
                    j = a[1]
                    nc.scalar.activation(xg_t[:, :, 2 * j * P:2 * (j + 1) * P], pair_view(), ACT.Copy)\
                        .then_inc(misc_free, 1)
                elif what == "lg":
                    nc.scalar.activation(lg_t[:, :], misc[:, 0:P], ACT.Copy).then_inc(misc_free, 1)
                elif what == "lt":
                    nc.scalar.activation(logits[:, bass.ds(b * TB + (a[0] * CT - TB), CT), :], logits_view(),
                                         ACT.Copy).then_inc(misc_free, 1)
                elif what == "ont":
                    for dc in range(DC):
                        last = nc.scalar.activation(o_t[:, dc, :], misc[:, dc * 2 * P:(dc + 1) * 2 * P],
                                                    ACT.Identity, bias=v_bias[:, dc:dc + 1])
                    last.then_inc(misc_free, 1)
                elif what == "mtr":
                    wait(eng, max_in[hg], lin(b, MAX_IN, MAX_IN))
                    nc.scalar.activation(max_t[:, :], misc16[0:HG * MROWS * TB, 0:P], ACT.Copy)\
                        .then_inc(misc_free, 1)

            def handle(b, n, hg, kind, *a):
                if kind == "st":
                    g, h = a
                    u = HG * g + h
                    off = group_shape(g)[2]
                    if h == 0:
                        wait(eng, pv_done, lin(b, NGRP * NG, NGRP * hg + g - 1))
                    eng.wait_ge(st_full, lin(b, NU * NG, NU * hg + u + 1))
                    nc.scalar.activation(probs[:, g % 2, h, 0:CW - off], st_bank[u % 3][:, 0:CW - off], ACT.Exp)\
                        .then_inc(exp_done, 1)
                elif kind == "oev":
                    c = a[0]
                    eng.wait_ge(pv_done, lin(b, NGRP * NG, NGRP * hg + (CT, 0)[c]))
                    nc.scalar.activation(o_raw[:, c * CW:(c + 1) * CW], o_bank[:, :], ACT.Copy).then_inc(o_out, 1)
                elif kind == "use":
                    evict(b, n, hg, *a)

            moe_scalar(0)
            walk(eng, handle)
            moe_scalar(1)

        @block.vector
        def _(eng):
            for bank in st_bank + s_bank + [o_bank, misc]:
                nc.vector.memset(bank[:, :], 0.0)
            nc.vector.memset(k_stack[KROWS:P, :, :, :], 1.0).then_inc(misc_free, 1)
            eng.wait_ge(weights_in, 16 * WEIGHT_DMAS)
            nc.vector.tensor_scalar(qk_bias[0:HG * HD, :], qk_bias[0:HG * HD, :], HD ** -0.5, None, ALU.mult)\
                .then_inc(consts_ready, 1)
            eng.wait_ge(consts_ready, CONSTS)

            with eng.Fori(0, NCH // 4) as i:
                for k in range(4):
                    c = i * 4 + k
                    tile = i * (4 * CT) + k * CT
                    eng.wait_ge(x_in[k], i * 16 + 16)
                    for t in range(CT):
                        vector_stats(t, tile + t)
                    vector_aggregate(eng).then_inc(stats_ready, 1)
                    eng.wait_ge(rstd_ready, c + 1)
                    eng.wait_ge(misc_free, c * 4 + 1)
                    for t in range(CT):
                        vector_normalise(t, tile + t).then_inc(xn_ready, 1)

            def top2_and_counts(layer, uses):
                eng.wait_ge(misc_free, uses + 1)
                vec = nc.vector
                wide = lambda ap: ap.to_broadcast([P, NT, E])
                eng.drain()
                vec.tensor_copy(left, logits[:, :, :])
                for choice in range(2):
                    eng.drain()
                    vec.tensor_reduce(top[:, :, 0], left, AX.X, ALU.max)
                    eng.drain()
                    vec.tensor_tensor(work, left, wide(top[:, :, :]), ALU.is_equal)
                    eng.drain()
                    vec.tensor_tensor(work, work, wide(rank[:, :, :]), ALU.mult)
                    eng.drain()
                    vec.tensor_reduce(best[:, :, 0], work, AX.X, ALU.max)
                    eng.drain()
                    vec.tensor_tensor(work, work, wide(best[:, :, :]), ALU.is_equal)
                    eng.drain()
                    if choice == 0:
                        vec.tensor_copy(chosen, work)
                        vec.scalar_tensor_tensor(out=left, in0=work, scalar=-BIG, in1=left, op0=ALU.mult,
                                                 op1=ALU.add)
                    else:
                        vec.tensor_tensor(chosen, chosen, work, ALU.add)
                eng.drain()
                vec.tensor_reduce(counts[:, :], chosen.rearrange("p t e -> p e t"), AX.X, ALU.add)\
                    .then_inc(counted, 1)
                eng.wait_ge(totalled, layer + 1)
                vec.tensor_scalar(kept[:, 0, :], total[:, :], float(CAP), None, ALU.is_le)
                eng.drain()
                vec.tensor_reduce(any_kept[:, :], kept[:, 0, :], AX.X, ALU.max)
                eng.drain()
                vec.tensor_copy(flag[:, :], any_kept[:, :]).then_inc(flag_ready, 1)

            def moe_vector(layer):
                vec = nc.vector
                wide = lambda ap: ap.to_broadcast([P, NT, E])

                def gate():
                    vec.tensor_reduce(top[:, :, 0], logits[:, :, :], AX.X, ALU.max)
                    eng.drain()
                    vec.tensor_tensor(left, logits[:, :, :], wide(top[:, :, :]), ALU.subtract)\
                        .then_inc(baton[layer], 1)
                    eng.wait_ge(baton[layer], 2)
                    vec.tensor_reduce(top[:, :, 0], work, AX.X, ALU.add)
                    eng.drain()
                    vec.reciprocal(best[:, :, :], top[:, :, :])
                    eng.drain()
                    vec.tensor_tensor(work, work, wide(best[:, :, :]), ALU.mult)
                    eng.drain()
                    vec.tensor_tensor(work, work, chosen, ALU.mult)
                    eng.drain()
                    vec.tensor_tensor(work, work, wide(kept[:, :, :]), ALU.mult)
                    eng.drain()
                    vec.tensor_scalar(work, work, 0.5, None, ALU.mult).then_inc(baton[layer], 1)

                def chunk(c):
                    eng.wait_ge(baton[layer], moe_value(c, None, 0))
                    for t in range(CT):
                        vector_stats(t, c * CT + t)
                    vector_aggregate(eng).then_inc(baton[layer], 1)
                    eng.wait_ge(baton[layer], moe_value(c, None, 2))
                    for t in range(CT):
                        last = vector_normalise(t, c * CT + t)
                    last.then_inc(baton[layer], 1)

                weight = probs[:, 0, 1, :]

                def expert(c, e):
                    eng.wait_ge(baton[layer], moe_value(c, e, 2))
                    vec.tensor_scalar(hidden_e, hidden_e, 1.0, None, ALU.add)
                    eng.drain()
                    vec.reciprocal(hidden_e, hidden_e)
                    eng.drain()
                    vec.tensor_tensor(hidden, hidden, hidden_e, ALU.mult).then_inc(baton[layer], 1)
                    eng.wait_ge(baton[layer], moe_value(c, e, 4))
                    for j in range(2):
                        vec.tensor_tensor(y_e[:, 2 * j:2 * j + 2, :],
                                          s_bank[j][:, :].rearrange("p (t d) -> p t d", t=2),
                                          b2_e.to_broadcast([P, 2, D]), ALU.add)
                    eng.drain()
                    for t in range(CT):
                        tile = x_tiles(c * CT + t, 1)[:, 0, :]
                        last = vec.scalar_tensor_tensor(out=tile, in0=y_e[:, t, :],
                                                        scalar=weight[:, bass.ds(c * (CT * E) + e + t * E, 1)],
                                                        in1=tile, op0=ALU.mult, op1=ALU.add)
                    last.then_inc(baton[layer], 1)

                moe_experts(eng, layer, gate, chunk, expert)

            def handle(b, n, hg, kind, *a):
                if kind == "s":
                    u = a[0]
                    ib, h, j0, width, diag = MAX_UNITS[u]
                    eng.wait_ge(s_full, lin(b, NU * NG, NU * (hg + 1) + u + 1))
                    if diag:
                        passed(eng, "vector")
                    bank = s_bank[u % 3][:, 0:width]
                    if diag:
                        nc.vector.tensor_tensor_reduce(out=bank, in0=bank, in1=causal[:, CW - width:CW],
                                                       scale=1.0, scalar=-BIG, op0=ALU.add, op1=ALU.max,
                                                       accum_out=max_diag[:, h, ib:ib + 1]).then_inc(max_done, 1)
                    else:
                        nc.vector.tensor_reduce(max_full[:, h, ib - CT:ib - CT + 1], bank, AX.X, ALU.max)\
                            .then_inc(max_done, 1)
                elif kind == "mfin":
                    eng.drain()
                    late = max_diag[:, :, CT:TB]
                    nc.vector.tensor_tensor(late, late, max_full[:, :, :], ALU.max)
                    eng.drain()
                    nc.vector.tensor_scalar(max_parts[:, 0, :, :], max_diag[:, :, :], -1.0, None, ALU.mult)
                    eng.drain()
                    nc.vector.scalar_tensor_tensor(out=max_rest[:, :, :], in0=max_diag[:, :, :], scalar=-1.0,
                                                   in1=max_parts[:, 0, :, :], op0=ALU.mult, op1=ALU.subtract)
                    eng.drain()
                    nc.vector.tensor_copy(max_parts[:, 1, :, :], max_rest[:, :, :])
                    eng.drain()
                    nc.vector.tensor_tensor(max_parts[:, 2, :, :], max_rest[:, :, :], max_parts[:, 1, :, :],
                                            ALU.subtract).then_inc(mparts_ready, 1)
                elif kind in ("lnstat", "lnnorm"):
                    what, c, t = a
                    tile = lin(b, TB, (TB if what == "x" else -TB) + c * CT + t)
                    if kind == "lnstat":
                        if t == 0:
                            eng.drain()
                        vector_stats(t, tile)
                    else:
                        if t == 0:
                            eng.wait_ge(rstd_ready, n("lnaggr"))
                            eng.wait_ge(misc_full, n("use"))
                        vector_normalise(t, tile).then_inc(xn_ready, 1)
                elif kind == "lnaggr":
                    vector_aggregate(eng).then_inc(stats_ready, 1)
                elif kind == "q2":
                    hq, c = a
                    m = hq if hg == 0 else hq + NG
                    eng.wait_ge(rest_ready, lin(b, 2 * NG, 2 * m + c + 1))
                    nc.vector.tensor_copy(parts[:, c, 1, :], rest[:, :]).then_inc(part2_ready, 1)
                elif kind == "use" and a[0] == "otr":
                    hq, c = a[1:]
                    eng.wait_ge(misc_full, n("use", 1))
                    heads = misc[:, :].rearrange("p (q w) -> p q w", w=32)
                    nc.vector.reciprocal(sum_inv[:, :, :], heads[:, :, HD:VW])
                    eng.drain()
                    nc.vector.tensor_tensor(
                        o_tok[:, c * CT:(c + 1) * CT, hq * HG * HD:(hq + 1) * HG * HD]
                        .rearrange("p t (h d) -> p t h d", h=HG),
                        heads[:, :, 0:HD].rearrange("p (t h) d -> p t h d", t=CT),
                        sum_inv[:, :, :].to_broadcast([P, CT * HG, HD])
                        .rearrange("p (t h) d -> p t h d", t=CT), ALU.mult).then_inc(misc_free, 1)
                elif kind == "use" and a[0] == "wo":
                    j = a[1]
                    eng.wait_ge(misc_full, n("use", 1))
                    eng.wait_ge(bo_added, lin(b, 4, j + 1 - 4))
                    now = x_tiles(b * TB + (2 * j - TB), 2)
                    nc.vector.tensor_tensor(now, misc[:, :].rearrange("p (t d) -> p t d", t=2), now, ALU.add)\
                        .then_inc(misc_free, 1)

            top2_and_counts(0, 4 * NCH)
            moe_vector(0)
            walk(eng, handle)
            top2_and_counts(1, COUNTS_AFTER["use"])
            moe_vector(1)

        @block.tensor
        def _(eng):
            eng.wait_ge(consts_ready, CONSTS)
            with eng.Fori(0, NCH) as c:
                for j in range(2):
                    if j == 0:
                        eng.wait_ge(xn_ready, c * CT + CT)
                    eng.wait_ge(misc_free, c * 4 + (j + 1))
                    tensor_transpose_tiles(misc, xn, 2 * j).then_inc(misc_full, 1)
                eng.wait_ge(misc_free, c * 4 + 3)
                tensor_gate_logits().then_inc(misc_full, 1)
                eng.wait_ge(misc_free, c * 4 + 4)
                nc.tensor.transpose(misc[:, 0:P], lg_t[:, :], ident[:, :]).then_inc(misc_full, 1)

            def moe_tensor(layer):
                def chunk(c):
                    eng.wait_ge(baton[layer], moe_value(c, None, 3))
                    for t in range(CT):
                        for dc in range(DC):
                            last = nc.tensor.transpose(st_bank[dc][:, t * P:(t + 1) * P],
                                                       xn[:, t, dc * P:(dc + 1) * P], ident[:, :])
                    last.then_inc(baton[layer], 1)

                def expert(c, e):
                    eng.wait_ge(baton[layer], moe_value(c, e, 0))
                    eng.wait_ge(moe_weights_in[layer], c * (64 * E) + e * 64 + 64)
                    for fc in range(DC):
                        for dc in range(DC):
                            last = nc.tensor.matmul(st_bank[fc][:, :], w1_e[:, dc, fc * P:(fc + 1) * P],
                                                    xg_t[:, dc, :], start=dc == 0, stop=dc == DC - 1)
                    last.then_inc(baton[layer], 1)
                    eng.wait_ge(baton[layer], moe_value(c, e, 3))
                    for t in range(CT):
                        for fc in range(DC):
                            last = nc.tensor.matmul(s_bank[t // 2][:, t % 2 * D:(t % 2 + 1) * D],
                                                    hidden[:, fc, t * P:(t + 1) * P], w2_e[:, fc, :],
                                                    start=fc == 0, stop=fc == DC - 1)
                    last.then_inc(baton[layer], 1)

                moe_experts(eng, layer, None, chunk, expert)

            def fill(b, n, hg, what, *a):
                wait(eng, misc_free, n("use", 1))
                if what == "v":
                    for t in range(2):
                        for dc in range(DC):
                            t0 = (2 * a[0] + t) * P
                            last = nc.tensor.matmul(misc[:, t * D:(t + 1) * D], x_t[:, dc, t0:t0 + P],
                                                    w_v[:, dc, :], start=dc == 0, stop=dc == DC - 1)
                elif what == "qk":
                    hq, c = a
                    for dc in range(DC):
                        last = nc.tensor.matmul(misc[:, :], w_qk[:, dc, hq, :], x_t[:, dc, c * CW:(c + 1) * CW],
                                                start=dc == 0, stop=dc == DC - 1)
                elif what in ("xt", "xg"):
                    eng.wait_ge(xn_ready, n("lnnorm"))
                    last = tensor_transpose_tiles(misc, xn, 2 * a[1])
                elif what == "lg":
                    last = tensor_gate_logits()
                elif what == "lt":
                    last = nc.tensor.transpose(misc[:, 0:P], lg_t[:, :], ident[:, :])
                elif what == "otr":
                    c = a[1]
                    eng.wait_ge(o_out, lin(b, 2 * NG, 2 * hg + c - 1))
                    for t in range(CT):
                        t0 = c * CW + t * P
                        last = nc.tensor.transpose(misc[:, t * P:(t + 1) * P], o_raw[:, t0:t0 + P], ident[:, :])
                elif what == "ont":
                    last = tensor_transpose_tiles(misc, o_tok, 2 * a[0])
                elif what == "wo":
                    for t in range(2):
                        for dc in range(DC):
                            last = nc.tensor.matmul(misc[:, t * D:(t + 1) * D], o_t[:, dc, t * P:(t + 1) * P],
                                                    w_o[:, dc, :], start=dc == 0, stop=dc == DC - 1)
                elif what == "mtr":
                    eng.wait_ge(mparts_ready, lin(b, NG, hg + 2))
                    last = nc.tensor.transpose(misc16[0:HG * MROWS * TB, 0:P],
                                               max_parts[:, :, :, :].rearrange("p k h t -> p (k h t)"),
                                               ident16[:, :])
                last.then_inc(misc_full, 1)

            def handle(b, n, hg, kind, *a):
                if kind == "st":
                    g, h = a
                    qc, jb, off, _ = group_shape(g)
                    u = HG * g + h
                    if u == 0:
                        eng.wait_ge(stack_in[hg], lin(b, STACK_IN, STACK_IN))
                        eng.wait_ge(max_in[hg], lin(b, MAX_IN, MAX_IN))
                    wait(eng, exp_done, lin(b, NU * NG, NU * hg + u - 2))
                    nc.tensor.matmul(st_bank[u % 3][:, 0:CW - off],
                                     k_stack[0:KROWS + MROWS, hg, h, jb * P:(jb + 1) * P],
                                     q_stack[0:KROWS + MROWS, hg, h, qc * CW + off:(qc + 1) * CW],
                                     start=True, stop=True).then_inc(st_full, 1)
                elif kind == "s":
                    u = a[0]
                    hm = (hg + 1) % NG
                    ib, h, j0, width, _ = MAX_UNITS[u]
                    if u == 0:
                        eng.wait_ge(stack_in[hm], lin(b, STACK_IN, STACK_IN * (2 if hm == 0 else 1)))
                    wait(eng, max_done, lin(b, NU * NG, NU * (hg + 1) + u - 2))
                    nc.tensor.matmul(s_bank[u % 3][:, 0:width], q_stack[0:KROWS, hm, h, ib * P:(ib + 1) * P],
                                     k_stack[0:KROWS, hm, h, j0:j0 + width], start=True, stop=True)\
                        .then_inc(s_full, 1)
                elif kind == "pv":
                    g = a[0]
                    back = g >= NGRP - 2
                    of = hg - back
                    _, jb, off, diag = group_shape(g)
                    if g == 0:
                        wait(eng, o_out, lin(b, 2 * NG, 2 * hg))
                        if hg == 0:
                            eng.wait_ge(misc_free, n("use", 1))
                    if g == CT:
                        eng.wait_ge(o_out, lin(b, 2 * NG, 2 * hg + 1))
                    if diag:
                        eng.wait_ge(sel_done, lin(b, 8 * NG, 8 * of + (g if g < CT else g - CT) + 1))
                    else:
                        eng.wait_ge(exp_done, lin(b, NU * NG, NU * of + HG * g + HG))
                    for h in range(HG):
                        last = nc.tensor.matmul(o_bank[32 * h:32 * h + VW, off:CW],
                                                v_aug[:, jb, of % NG * HG + h, :],
                                                probs[:, g % 2, h, 0:CW - off], start=g in (0, CT),
                                                stop=g in (CT - 1, NGRP - 1))
                    last.then_inc(pv_done, 1)
                elif kind == "use":
                    fill(b, n, hg, *a)

            moe_tensor(0)
            walk(eng, handle)
            moe_tensor(1)


_OUT_SHAPE = (NT, P, D)


def kernel(L0_attn_x, L0_attn_Wq, L0_attn_bq, L0_attn_Wkv, L0_attn_bkv, L0_attn_Wo, L0_attn_bo,
           L0_ffn_gate_w, L0_ffn_w1, L0_ffn_b1, L0_ffn_w2, L0_ffn_b2):
    import numpy as np
    import concourse.bacc as bacc
    from concourse.bass_utils import run_bass_kernel_spmd

    def grouped(q, k):
        parts = [p.reshape(p.shape[:-1] + (NG, HG, HD)).swapaxes(-1, -2).reshape(p.shape[:-1] + (NG, HG * HD))
                 for p in (q, k)]
        return np.concatenate(parts, axis=-1)

    a = {n: np.asarray(v) for n, v in locals().items() if n.startswith("L0_")}
    wk, wv = a["L0_attn_Wkv"][:D], a["L0_attn_Wkv"][D:]
    arrays = {
        "x": a["L0_attn_x"].reshape(_OUT_SHAPE),
        "wqk_t": grouped(a["L0_attn_Wq"].T, wk.T),
        "wv_t": wv.T,
        "wo_t": a["L0_attn_Wo"].T,
        "bqk": grouped(a["L0_attn_bq"], a["L0_attn_bkv"][:D]),
        "bv": a["L0_attn_bkv"][D:],
        "bo": a["L0_attn_bo"],
        "gate_t": a["L0_ffn_gate_w"].T,
        "w1_t": a["L0_ffn_w1"].transpose(0, 2, 1),
        "b1": a["L0_ffn_b1"],
        "w2_t": a["L0_ffn_w2"].transpose(0, 2, 1),
        "b2": a["L0_ffn_b2"],
    }
    arrays = {n: np.ascontiguousarray(v) for n, v in arrays.items()}
    nc = bacc.Bacc("TRN2", target_bir_lowering=False, num_devices=1)
    nc.disable_value_cache = True
    args = [nc.dram_tensor(n, v.shape, mybir.dt.from_np(v.dtype), kind="ExternalInput").ap()
            for n, v in arrays.items()]
    out = nc.dram_tensor("out", _OUT_SHAPE, FP32, kind="ExternalOutput").ap()
    program(nc, *args, out)
    r = run_bass_kernel_spmd(nc, [arrays], core_ids=[0])
    return r.results[0]["out"].reshape(B, S, D)
```

```python
import struct

import concourse.bass as bass
from concourse import mybir
from contextlib import ExitStack

FP32 = mybir.dt.float32
BF16 = mybir.dt.bfloat16
INT32 = mybir.dt.int32
ALU = mybir.AluOpType
ACT = mybir.ActivationFunctionType
AX = mybir.AxisListType
ADD_REDUCE = bass.bass_isa.ReduceOp.add

B, S, D = 8, 1024, 256
H, HD = 16, 16
HG, NG = 4, 4
P = 128
TB = S // P
NT = B * TB
DC = D // P
CW = 512
CT = CW // P
NCH = B * S // CW
LOADS = 4
E = 8
CAP = int(1.25 * B * S / E)
EPS = 1e-5
KROWS = 6 * HD
MROWS = 3
VW = HD + 1
BIG = 3.0e38
TWO_ONES = struct.unpack("<f", struct.pack("<I", 0x3F803F80))[0]
NU = 48
Q2_LAG = 3
NORM_LAG = 9
NGRP = NU // HG
RUNS = ((0, 3, 0), (3, 2, 1), (5, 1, 2))
STACK_DMAS = 2 * len(RUNS)


EARLY = 3


def group_shape(g):
    if g < CT:
        return 0, g, g * P, True
    jb = g - CT
    return 1, jb, max(0, jb - CT) * P, jb >= CT


def max_units():
    full = [(ib, h, 0, CW, False) for ib in range(CT, TB) for h in range(HG)]
    diag = [(ib, h, ib // CT * CW, (ib % CT + 1) * P, True) for ib in range(TB) for h in range(HG)]
    out = []
    for i, f in enumerate(full):
        out += [f, diag[2 * i], diag[2 * i + 1]]
    return out


MAX_UNITS = max_units()


def step_plan(hg, prev, nxt):
    extra = {}

    def put(u, *events):
        extra.setdefault(u, []).extend(events)

    def norm_jobs(kind, c, u):
        for t in range(CT):
            put(u + t, ("lnstat", kind, c, t))
            put(u + NORM_LAG + t, ("lnnorm", kind, c, t))
        put(u + CT, ("lnaggr", kind, c))

    def project(hq, *units):
        for c, u in enumerate(units):
            put(u, ("use", "qk", hq, c))
            put(u + Q2_LAG, ("q2", hq, c))
            put(u + Q2_LAG + 2, ("q3", hq, c))

    def gate_jobs(c, u):
        norm_jobs("g", c, u)
        for i, what in enumerate((("xg", c, 0), ("xg", c, 1))):
            put(u + NORM_LAG + 6 + 4 * i, ("use",) + what)
        put(u + NORM_LAG + 18, ("use", "lg", c))
        put(u + NORM_LAG + 24, ("use", "lt", c))

    if hg == 0:
        for j, u in enumerate((5, 9, 18, 21)):
            put(u, ("use", "v", j))
        if prev:
            put(1, ("use", "otr", 3, 0))
            put(12, ("use", "otr", 3, 1))
        project(3, 15, 24)
        if nxt:
            norm_jobs("x", 0, 8)
            put(27, ("use", "xt", 0, 0))
            put(30, ("use", "xt", 0, 1))
            norm_jobs("x", 1, 24)
            put(38, ("use", "xt", 1, 0))
            put(44, ("use", "xt", 1, 1))
    if hg == 1:
        for i, u in enumerate((8, 20, 28, 36)):
            put(u, ("bo", i))
        if prev:
            for j, (u, v) in enumerate(((1, 7), (10, 16), (20, 26), (30, 36))):
                put(u, ("use", "ont", j))
                put(v, ("use", "wo", j))
            put(38, ("out",))
        put(13, ("use", "otr", 0, 0))
        put(33, ("use", "otr", 0, 1))
        if nxt:
            project(0, 4, 23)
    if hg >= 2:
        put(1, ("use", "otr", hg - 1, 0))
        put(9, ("use", "otr", hg - 1, 1))
        if prev:
            gate_jobs(hg - 2, 4)
        if nxt:
            project(hg - 1, 5, 26)
    if hg < NG - 1 or nxt:
        put(NU - HG * EARLY, ("mfin",))
        put(NU - HG * EARLY + 5, ("use", "mtr"), ("mdma",))
    plan = []
    for g in range(NGRP):
        for h in range(HG):
            plan.append(("st", g, h))
            if h == 0 and not (hg == 0 and not prev and g < 2):
                plan.append(("pv", (g - 2) % NGRP))
                if g == 1:
                    plan.append(("oev", 1))
                if g == CT + 1:
                    plan.append(("oev", 0))
            u = HG * (g + EARLY) + h
            ahead = 1 + u // NU
            if hg + ahead < NG or nxt:
                plan.append(("s", ahead, u % NU))
            plan += extra.get(HG * g + h, [])
    return [(hg,) + e for e in plan]


def batch_plan(prev, nxt):
    return [e for hg in range(NG) for e in step_plan(hg, prev, nxt)]


def prologue_plan():
    plan = []

    def project(hq, c):
        return [(3, "use", "qk", hq, c), (3, "q2", hq, c), (3, "q3", hq, c)]

    plan += project(0, 0) + project(0, 1) + project(1, 0) + project(1, 1)
    for u in range(NU):
        plan += [(3, "s", 1, u)]
        for i, c in ((8, 0), (22, 1)):
            if u in (i, i + 7, i + 9):
                plan += [project(2, c)[(0, 7, 9).index(u - i)]]
    plan += [(3, "mfin",)]
    for u in range(HG * EARLY):
        plan += [(3, "s", 2, u)]
        if u == 3:
            plan += [(3, "use", "mtr"), (3, "mdma",)]
    return plan


def epilogue_plan():
    plan = [(0, "pv", NGRP - 2), (0, "pv", NGRP - 1), (0, "oev", 1)] + [(0, "use", "otr", 3, c) for c in range(2)]
    for j in range(4):
        plan += [(0, "use", "ont", j), (0, "use", "wo", j)]
    plan += [(0, "out")]
    for c in range(2):
        plan += [(0, "lnstat", "g", c, t) for t in range(CT)] + [(0, "lnaggr", "g", c)]
        plan += [(0, "lnnorm", "g", c, t) for t in range(CT)]
        plan += [(0, "use", "xg", c, j) for j in range(2)] + [(0, "use", "lg", c), (0, "use", "lt", c)]
    return plan


def count(plan, kind):
    return sum(e[1] == kind for e in plan)


def make_sections():
    before = {"use": 0, "lnaggr": NCH, "lnnorm": CT * NCH}
    out = []
    for plan, times, b in ((prologue_plan(), 1, -1), (batch_plan(False, True), 1, 0),
                           (batch_plan(True, True), B - 2, 1), (batch_plan(True, False), 1, B - 1),
                           (epilogue_plan(), 1, B)):
        out.append((plan, times, b, dict(before)))
        for k in before:
            before[k] += times * count(plan, k)
    return out, before


SECTIONS, COUNTS_AFTER = make_sections()


def walk(eng, handle):
    for plan, times, b0, start in SECTIONS:
        def events(b):
            seen = dict.fromkeys(start, 0)
            for hg, kind, *a in plan:
                def n(k, more=0):
                    if times == 1:
                        return start[k] + seen[k] + more
                    per = count(plan, k)
                    return b * per + (start[k] + seen[k] + more - per * b0)
                handle(b, n, hg, kind, *a)
                if kind in seen:
                    seen[kind] += 1
        if times == 1:
            events(b0)
        else:
            with eng.Fori(b0, b0 + times) as b:
                events(b)


def wait(eng, sem, value):
    if not isinstance(value, int) or value > 0:
        eng.wait_ge(sem, value)


def program(nc, x, wqk_t, wv_t, wo_t, bqk, bv, bo, gate_t, w1_t, b1, w2_t, b2, out):
    with ExitStack() as ctx:
        ctx.enter_context(nc.allow_non_contiguous_dma(reason="biases and gate columns"))

        def sb(name, shape, dt=FP32):
            return ctx.enter_context(nc.sbuf_tensor(name, shape, dt))

        def pb(name):
            return ctx.enter_context(nc.psum_tensor(name, [P, CW], FP32))

        def sem(name):
            return ctx.enter_context(nc.semaphore(name))

        x_all = sb("x_all", [P, NT, D])
        w_qk = sb("w_qk", [P, DC, NG, P])
        w_v = sb("w_v", [P, DC, D])
        w_o = sb("w_o", [P, DC, D])
        w_gate = sb("w_gate", [P, DC, 32])
        qk_bias = sb("qk_bias", [P, NG])
        qk_scale = sb("qk_scale", [P, 1])
        v_bias = sb("v_bias", [P, DC])
        bo_row = sb("bo_row", [P, 1, D])
        ident = sb("ident", [P, P])
        ident16 = sb("ident16", [P, P], BF16)
        causal = sb("causal", [P, CW], BF16)
        neg_half = sb("neg_half", [P, CT])
        stats = sb("stats", [P, CT, 6])
        mean_var = sb("mean_var", [P, CT, 2])
        rstd = sb("rstd", [P, CT])
        xn = sb("xn", [P, CT, D])
        x_t = sb("x_t", [P, DC, S])
        xg_t = sb("xg_t", [P, DC, CW])
        qk32 = sb("qk32", [P, CW])
        rest = sb("rest", [P, CW])
        parts = sb("parts", [P, 2, 3, CW], BF16)
        q_stack = sb("q_stack", [P, NG, HG, S], BF16)
        k_stack = sb("k_stack", [P, NG, HG, S], BF16)
        v_aug = sb("v_aug", [P, TB, H, VW])
        probs = sb("probs", [P, 2, HG, CW])
        o_raw = sb("o_raw", [P, S])
        sum_inv = sb("sum_inv", [P, CT * HG, 1])
        o_tok = sb("o_tok", [P, TB, D])
        o_t = sb("o_t", [P, DC, 2 * P])
        max_diag = sb("max_diag", [P, HG, TB])
        max_full = sb("max_full", [P, HG, CT])
        max_rest = sb("max_rest", [P, HG, TB])
        max_parts = sb("max_parts", [P, MROWS, HG, TB], BF16)
        max_t = sb("max_t", [HG * MROWS * TB, P], BF16)
        lg_t = sb("lg_t", [P, P])
        logits = sb("logits", [P, NT, E])
        rank = sb("rank", [P, 1, E])
        top = sb("top", [P, NT, 1])
        best = sb("best", [P, NT, 1])
        counts = sb("counts", [P, E])
        total = sb("total", [P, E])
        kept = sb("kept", [P, 1, E])
        any_kept = sb("any_kept", [P, 1])
        flag = sb("flag", [P, 1], INT32)
        chosen, work, left = (probs[:, 0, i, :].rearrange("p (t e) -> p t e", e=E) for i in range(3))
        gate_xn = (xn[:, :, :], probs[:, 1, 0:2, :].rearrange("p a (t d) -> p (a t) d", d=D))
        gate_xt = (xg_t[:, :, :], o_tok[:, :, :].rearrange("p (c t) d -> p c (t d)", c=DC)[:, :, 0:CW])
        gate_lg = (lg_t[:, :], rest[:, 0:P])
        moe_space = q_stack[:, :, :, :].rearrange("p g h s -> p (g h s)").bitcast(FP32)
        w1_e = moe_space[:, 0:512].rearrange("p (c f) -> p c f", c=DC)
        w2_e = moe_space[:, 512:1024].rearrange("p (c f) -> p c f", c=DC)
        b2_e = moe_space[:, 1024:1280].rearrange("p (t f) -> p t f", t=1)
        b1_e = moe_space[:, 1280:1282]
        hidden = moe_space[:, 2048:3072].rearrange("p (c t) -> p c t", c=DC)
        hidden_e = moe_space[:, 3072:4096].rearrange("p (c t) -> p c t", c=DC)
        y_e = moe_space[:, 4096:5120].rearrange("p (t f) -> p t f", t=CT)

        st_bank = [pb(f"st{i}") for i in range(3)]
        s_bank = [pb(f"s{i}") for i in range(3)]
        o_bank = pb("o_bank")
        misc = pb("misc")
        misc16 = misc[:, :].bitcast(BF16)
        gate_bank = ((*st_bank, s_bank[0]), (s_bank[1], s_bank[2], o_bank, misc))

        part_dram = nc.dram_tensor("part_dram", [NG, 2, 3, HG * HD, S], BF16, kind="Internal").ap()

        weights_in = sem("weights_in")
        gate_weight_in = sem("gate_weight_in")
        bias_scaled = sem("bias_scaled")
        consts_ready = sem("consts_ready")
        consts_step = sem("consts_step")
        x_in = [sem(f"x_in{i}") for i in range(LOADS)]
        misc_full = sem("misc_full")
        misc_free = sem("misc_free")
        stats_ready = sem("stats_ready")
        rstd_ready = sem("rstd_ready")
        xn_ready = sem("xn_ready")
        rest_ready = sem("rest_ready")
        part2_ready = sem("part2_ready")
        part3_ready = sem("part3_ready")
        parts_out = [sem(f"parts_out{i}") for i in range(2)]
        stack_in = [sem(f"stack_in{i}") for i in range(NG)]
        st_full = sem("st_full")
        exp_done = sem("exp_done")
        sel_done = sem("sel_done")
        pv_done = sem("pv_done")
        o_out = sem("o_out")
        s_full = sem("s_full")
        max_done = sem("max_done")
        mparts_ready = sem("mparts_ready")
        max_in = [sem(f"max_in{i}") for i in range(NG)]
        bo_added = sem("bo_added")
        out_written = sem("out_written")
        counted = sem("counted")
        totalled = sem("totalled")
        flag_ready = sem("flag_ready")
        baton = [sem(f"baton{i}") for i in range(2)]
        moe_weights_in = [sem(f"moe_weights_in{i}") for i in range(2)]

        wait_passed = {name: sem(f"wait_passed_{name}") for name in ("sync", "gpsimd", "vector")}

        WEIGHT_DMAS = 6
        CONSTS = 2
        MIDDLE = B - 2
        STACK_IN, MAX_IN = 16 * STACK_DMAS, 16
        GATE_TURNS, CHUNK_TURNS, EXPERT_TURNS = 3, 5, 5
        TURNS = CHUNK_TURNS + E * EXPERT_TURNS

        def lin(b, k, c):
            return b * k + c

        def passed(eng, name):
            eng.sem_inc(wait_passed[name], 1)

        def x_tiles(t0, n):
            return x_all[:, bass.ds(t0, n), :]

        def row_out(t, width):
            return misc[:, t * width:(t + 1) * width]

        def vector_stats(t, tile):
            nc.vector.bn_stats(stats[:, t, :], x_tiles(tile, 1)[:, 0, :])

        def vector_aggregate(eng):
            eng.drain()
            for t in range(CT):
                last = nc.vector.bn_aggr(mean_var[:, t, :], stats[:, t, :])
            return last

        def vector_normalise(t, tile, dst=xn):
            return nc.vector.tensor_scalar(dst[:, t, :], x_tiles(tile, 1)[:, 0, :], mean_var[:, t, 0:1],
                                           rstd[:, t:t + 1], ALU.subtract, ALU.mult)

        def pool_rstd(eng, fenced, value):
            nc.gpsimd.tensor_scalar_add(rstd[:, :], mean_var[:, :, 1], EPS).then_inc(fenced, 1)
            eng.wait_ge(fenced, value)
            return nc.gpsimd.tensor_tensor(rstd[:, :], rstd[:, :], neg_half[:, :], ALU.pow)

        rstd_sum = sem("rstd_sum")
        gate_xt_full = sem("gate_xt_full")
        gate_xt_taken = sem("gate_xt_taken")
        gate_lg_full = sem("gate_lg_full")
        gate_lg_taken = sem("gate_lg_taken")
        gate_lt_full = sem("gate_lt_full")
        gate_lt_taken = sem("gate_lt_taken")

        def gate_xt_of(chunk, odd):
            if isinstance(chunk, int) and chunk < S // CW:
                return x_t[:, :, chunk * CW:(chunk + 1) * CW]
            return gate_xt[odd]

        def gate_pipeline(eng, stages, body):
            def peeled(i):
                body(i % LOADS, {k: i - k for k in range(stages) if 0 <= i - k < NCH})
            for i in range(LOADS):
                peeled(i)
            with eng.Fori(1, NCH // LOADS) as four:
                for slot in range(LOADS):
                    body(slot, {k: four * LOADS + (slot - k) for k in range(stages)})
            for i in range(NCH, NCH + stages - 1):
                peeled(i)

        moe_rstd_sum = [sem(f"moe_rstd_sum{i}") for i in range(2)]

        def tensor_gate_logits(bank, xt):
            for dc in range(DC):
                for t in range(CT):
                    last = nc.tensor.matmul(bank[32 * t:32 * t + 32, 0:P], w_gate[:, dc, :],
                                            xt[:, dc, t * P:(t + 1) * P], start=dc == 0, stop=dc == DC - 1)
            return last

        def tensor_transpose_tiles(dst, src, t0):
            for dc in range(DC):
                for t in range(2):
                    i = 2 * dc + t
                    last = nc.tensor.transpose(dst[:, i * P:(i + 1) * P],
                                               src[:, t0 + t, dc * P:(dc + 1) * P], ident[:, :])
            return last

        def pair_view(bank):
            return bank[:, :].rearrange("p (c t) -> p c t", c=DC)

        def logits_view(bank):
            return bank[:, 0:P].rearrange("p (t e) -> p t e", t=CT)[:, :, 0:E]

        def moe_value(c, e, turn):
            if e is None:
                return c * TURNS + (GATE_TURNS + turn)
            return c * TURNS + (e * EXPERT_TURNS + (GATE_TURNS + CHUNK_TURNS + turn))

        def moe_experts(eng, layer, gate, chunk, expert):
            eng.wait_ge(flag_ready, layer + 1)
            kept_here = eng.value_load(flag[0:1, 0:1], min_val=0, max_val=1)
            with eng.If(kept_here > 0):
                if gate:
                    gate()
                with eng.Fori(0, NCH) as c:
                    if chunk:
                        chunk(c, c, lambda turn: moe_value(c, None, turn))
                    with eng.Fori(0, E) as e:
                        expert(c, e)
                done = GATE_TURNS + NCH * TURNS
                if layer == 0:
                    for c in range(S // CW):
                        if chunk:
                            chunk(c, NCH + c, lambda turn: done + turn)
                        done += CHUNK_TURNS
                eng.wait_ge(baton[layer], done)
            with eng.Else():
                eng.nop()

        block = ctx.enter_context(nc.Block())

        @block.sync
        def _(eng):
            for k in range(LOADS):
                eng.dma_start(x_tiles(k * CT, CT), x[k * CT:(k + 1) * CT, :, :].rearrange("t p d -> p t d"))\
                   .then_inc(x_in[k], 16)
            with eng.Fori(1, NCH // LOADS) as i:
                for k in range(LOADS):
                    eng.wait_ge(x_in[k], i * 16)
                    passed(eng, "sync")
                    eng.dma_start(x_tiles(i * (LOADS * CT) + k * CT, CT),
                                  x[bass.ds(i * (LOADS * CT) + k * CT, CT), :, :].rearrange("t p d -> p t d"))\
                       .then_inc(x_in[k], 16)

            def moe_sync(layer):
                def expert(c, e):
                    eng.wait_ge(baton[layer], moe_value(c, e, 0))
                    passed(eng, "sync")
                    for dst, src in ((w1_e, w1_t[bass.ds(e, 1), :, :].rearrange("e (c p) f -> p (e c) f", p=P)),
                                     (w2_e, w2_t[bass.ds(e, 1), :, :].rearrange("e (c p) f -> p (e c) f", p=P)),
                                     (b1_e, b1[bass.ds(e, 1), :].rearrange("e (c p) -> p (e c)", p=P)),
                                     (b2_e, b2[bass.ds(e, 1), :].partition_broadcast(P))):
                        eng.dma_start(dst, src).then_inc(moe_weights_in[layer], 16)
                moe_experts(eng, layer, None, None, expert)

            def handle(b, n, hg, kind, *a):
                if kind == "q3":
                    hq, c = a
                    m = (4, hq if hg == 0 else hq + NG)
                    eng.wait_ge(part3_ready, lin(b, 2 * m[0], 2 * m[1] + c + 1))
                    passed(eng, "sync")
                    if c == 0:
                        wait(eng, stack_in[hq], lin(b, STACK_IN, 0 if hg == 0 else STACK_IN))
                    for qk in range(2):
                        eng.dma_start(part_dram[hq, qk, :, :, c * CW:(c + 1) * CW].rearrange("k p c -> p k c"),
                                      parts[qk * HG * HD:(qk + 1) * HG * HD, c, :, :]).then_inc(parts_out[c], 16)
                    if c == 1:
                        for half in range(2):
                            eng.wait_ge(parts_out[half], lin(b, 32 * m[0], 32 * m[1] + 32))
                            passed(eng, "sync")
                        wait(eng, pv_done, lin(b, NGRP * m[0], NGRP * (m[1] - 3)))
                        for r, times, part in RUNS:
                            rows = slice(r * HD, (r + times) * HD)
                            eng.dma_start(q_stack[rows, hq, :, :].rearrange("r h c -> r (h c)"),
                                          part_dram[hq, 0, 0:times, :, :].rearrange("k (d h) c -> (k d) (h c)", h=HG))\
                               .then_inc(stack_in[hq], 16)
                            eng.dma_start(k_stack[rows, hq, :, :].rearrange("r h c -> r (h c)"),
                                          part_dram[hq, 1, part, :, :].rearrange("(d h) c -> d (h c)", h=HG)
                                          .partition_broadcast(times)).then_inc(stack_in[hq], 16)
                elif kind == "mdma":
                    hm = (hg + 1) % NG
                    eng.wait_ge(misc_free, n("use", 1))
                    eng.dma_start(q_stack[KROWS:KROWS + MROWS, hm, :, :].rearrange("k h (t c) -> k (h t) c", c=P),
                                  max_t[:, :]).then_inc(max_in[hm], 16)
                elif kind == "out":
                    eng.wait_ge(misc_free, n("use", 1))
                    passed(eng, "sync")
                    eng.dma_start(out[bass.ds(b * TB - TB, TB), :, :].rearrange("t p d -> p t d"),
                                  x_tiles(b * TB - TB, TB)).then_inc(out_written, 16)

            moe_sync(0)
            walk(eng, handle)
            eng.wait_ge(out_written, 16 * B)
            moe_sync(1)
            with eng.If(eng.value_load(flag[0:1, 0:1], min_val=0, max_val=1) > 0):
                eng.dma_start(out.rearrange("t p d -> p t d"), x_all[:, :, :]).then_inc(out_written, 16)
                eng.wait_ge(out_written, 16 * B + 16)
            with eng.Else():
                eng.nop()

        @block.gpsimd
        def _(eng):
            nc.gpsimd.memset(ident[:, :], 0.0)
            nc.gpsimd.memset(causal[:, :], 0.0)
            nc.gpsimd.memset(w_gate[:, :, E:32], 0.0)
            nc.gpsimd.memset(neg_half[:, :], -0.5)
            nc.gpsimd.memset(qk_scale[:, :], 1.0).then_inc(consts_step, 1)
            eng.wait_ge(consts_step, 1)
            nc.gpsimd.affine_select(out=ident[:, :], in_=ident[:, :], compare_op=ALU.not_equal, fill=1.0,
                                    base=0, pattern=[[-1, P]], channel_multiplier=1)
            nc.gpsimd.affine_select(out=causal[:, CW - P:CW], in_=causal[:, CW - P:CW], compare_op=ALU.is_ge,
                                    fill=-BIG, base=0, pattern=[[-1, P]], channel_multiplier=1)
            nc.gpsimd.memset(qk_scale[0:HG * HD, :], HD ** -0.5)
            for e in range(E):
                nc.gpsimd.memset(rank[:, 0, e:e + 1], float(E - e))
            nc.gpsimd.memset(v_aug[:, :, :, HD:VW], 1.0).then_inc(consts_step, 1)
            eng.wait_ge(consts_step, 2)
            nc.gpsimd.tensor_copy(ident16[:, :], ident[:, :]).then_inc(consts_ready, 1)

            with eng.Fori(0, NCH) as c:
                eng.wait_ge(stats_ready, c + 1)
                passed(eng, "gpsimd")
                pool_rstd(eng, rstd_sum, c + 1).then_inc(rstd_ready, 1)

            def moe_pool(layer):
                eng.wait_ge(counted, layer + 1)
                nc.gpsimd.partition_all_reduce(total[:, :], counts[:, :], P, ADD_REDUCE).then_inc(totalled, 1)

                def chunk(c, i, turn):
                    eng.wait_ge(baton[layer], turn(1))
                    passed(eng, "gpsimd")
                    pool_rstd(eng, moe_rstd_sum[layer], i + 1).then_inc(baton[layer], 1)

                moe_experts(eng, layer, None, chunk, lambda c, e: eng.nop())

            def handle(b, n, hg, kind, *a):
                if kind == "st":
                    g, h = a
                    if h == HG - 1 and group_shape(g)[3]:
                        eng.wait_ge(exp_done, lin(b, NU * NG, NU * hg + HG * g + HG))
                        passed(eng, "gpsimd")
                        now = probs[:, g % 2, :, 0:P]
                        nc.gpsimd.affine_select(out=now, in_=now, compare_op=ALU.is_ge, fill=0.0, base=0,
                                                pattern=[[0, HG], [1, P]], channel_multiplier=-1)\
                            .then_inc(sel_done, 1)
                elif kind == "lnaggr":
                    eng.wait_ge(stats_ready, n("lnaggr", 1))
                    passed(eng, "gpsimd")
                    pool_rstd(eng, rstd_sum, n("lnaggr", 1)).then_inc(rstd_ready, 1)
                elif kind == "use" and a[0] == "qk":
                    hq, c = a[1:]
                    m = hq if hg == 0 else hq + NG
                    wait(eng, part3_ready, lin(b, 2 * NG, 2 * m + c))
                    eng.wait_ge(misc_free, n("use", 2))
                    nc.gpsimd.tensor_tensor(rest[:, :], qk32[:, :], parts[:, c, 0, :], ALU.subtract)\
                        .then_inc(rest_ready, 1)
                elif kind == "q3":
                    hq, c = a
                    m = hq if hg == 0 else hq + NG
                    eng.wait_ge(part2_ready, lin(b, 2 * NG, 2 * m + c + 1))
                    nc.gpsimd.tensor_tensor(parts[:, c, 2, :], rest[:, :], parts[:, c, 1, :], ALU.subtract)\
                        .then_inc(part3_ready, 1)
                elif kind == "bo":
                    eng.wait_ge(xn_ready, n("lnnorm"))
                    now = x_tiles(b * TB + 2 * a[0], 2)
                    nc.gpsimd.tensor_tensor(now, now, bo_row[:, :, :].to_broadcast([P, 2, D]), ALU.add)\
                        .then_inc(bo_added, 1)

            eng.wait_ge(rstd_ready, NCH)
            nc.gpsimd.memset(k_stack[P // 2:P, :, :, :].rearrange("p g h s -> p (g h s)").bitcast(FP32), TWO_ONES)\
                .then_inc(misc_free, 1)
            eng.wait_ge(weights_in, 16 * WEIGHT_DMAS)
            eng.wait_ge(misc_free, 1)
            moe_pool(0)
            walk(eng, handle)
            moe_pool(1)

        @block.scalar
        def _(eng):
            eng.dma_start(w_gate[:, :, 0:E], gate_t.rearrange("(c p) e -> p c e", p=P)).then_inc(gate_weight_in, 16)
            for dst, src in ((w_qk[:, :, :, :], wqk_t.rearrange("(c p) g f -> p c g f", p=P)),
                             (w_v[:, :, :], wv_t.rearrange("(c p) f -> p c f", p=P)),
                             (w_o[:, :, :], wo_t.rearrange("(c p) f -> p c f", p=P)),
                             (qk_bias[:, :], bqk.rearrange("g p -> p g")),
                             (v_bias[:, :], bv.rearrange("(c p) -> p c", p=P)),
                             (bo_row[:, :, :], bo.rearrange("(t d) -> t d", t=1).partition_broadcast(P))):
                eng.dma_start(dst, src).then_inc(weights_in, 16)

            def gate_round(slot, chunk):
                odd = slot % 2
                if 0 in chunk:
                    wait(eng, gate_lg_full, chunk[0] - 1)
                    for j in range(2):
                        eng.wait_ge(gate_xt_full, chunk[0] * 2 + (j + 1))
                        nc.scalar.activation(gate_xt_of(chunk[0], odd)[:, :, 2 * j * P:2 * (j + 1) * P],
                                             pair_view(gate_bank[odd][j]), ACT.Copy).then_inc(gate_xt_taken, 1)
                if 1 in chunk:
                    eng.wait_ge(gate_lg_full, chunk[1] + 1)
                    wait(eng, gate_lt_full, chunk[1] - 1)
                    nc.scalar.activation(gate_lg[1 - odd], gate_bank[1 - odd][2][:, 0:P], ACT.Copy)\
                        .then_inc(gate_lg_taken, 1)
                if 2 in chunk:
                    eng.wait_ge(gate_lt_full, chunk[2] + 1)
                    nc.scalar.activation(logits[:, bass.ds(chunk[2] * CT, CT), :], logits_view(gate_bank[odd][3]),
                                         ACT.Copy).then_inc(gate_lt_taken, 1)

            gate_pipeline(eng, 3, gate_round)

            def moe_scalar(layer):
                def gate():
                    eng.wait_ge(baton[layer], 1)
                    nc.scalar.activation(work, left, ACT.Exp).then_inc(baton[layer], 1)

                def chunk(c, i, turn):
                    eng.wait_ge(baton[layer], turn(4))
                    for dc in range(DC):
                        dst = xg_t[:, dc, :] if i is c else x_t[:, dc, c * CW:(c + 1) * CW]
                        last = nc.scalar.activation(dst, st_bank[dc][:, :], ACT.Copy)
                    last.then_inc(baton[layer], 1)

                def expert(c, e):
                    eng.wait_ge(baton[layer], moe_value(c, e, 1))
                    for fc in range(DC):
                        nc.scalar.activation(hidden[:, fc, :], st_bank[fc][:, :], ACT.Identity,
                                             bias=b1_e[:, fc:fc + 1])
                    eng.drain()
                    nc.scalar.activation(hidden_e, hidden, ACT.Exp, scale=-1.0).then_inc(baton[layer], 1)

                moe_experts(eng, layer, gate, chunk, expert)

            def evict(b, n, hg, what, *a):
                if what in ("otr", "wo"):
                    return
                eng.wait_ge(misc_full, n("use", 1))
                if what == "v":
                    j = a[0]
                    nc.scalar.activation(v_aug[:, 2 * j:2 * j + 2, :, 0:HD],
                                         misc[:, :].rearrange("p (t h d) -> p t h d", t=2, d=HD), ACT.Copy)\
                        .then_inc(misc_free, 1)
                elif what == "qk":
                    hq, c = a
                    m = hq if hg == 0 else hq + NG
                    wait(eng, parts_out[c], lin(b, 32 * NG, 32 * m))
                    wait(eng, rest_ready, lin(b, 2 * NG, 2 * m + c))
                    for dst in (qk32[:, :], parts[:, c, 0, :]):
                        last = nc.scalar.activation(dst, misc[:, :], ACT.Identity, bias=qk_bias[:, hq:hq + 1],
                                                    scale=qk_scale[:, :])
                    last.then_inc(misc_free, 1)
                elif what == "xt":
                    c, j = a
                    t0 = c * CW + 2 * j * P
                    nc.scalar.activation(x_t[:, :, t0:t0 + 2 * P], pair_view(misc), ACT.Copy).then_inc(misc_free, 1)
                elif what == "xg":
                    j = a[1]
                    nc.scalar.activation(xg_t[:, :, 2 * j * P:2 * (j + 1) * P], pair_view(misc), ACT.Copy)\
                        .then_inc(misc_free, 1)
                elif what == "lg":
                    nc.scalar.activation(lg_t[:, :], misc[:, 0:P], ACT.Copy).then_inc(misc_free, 1)
                elif what == "lt":
                    nc.scalar.activation(logits[:, bass.ds(b * TB + (a[0] * CT - TB), CT), :], logits_view(misc),
                                         ACT.Copy).then_inc(misc_free, 1)
                elif what == "ont":
                    for dc in range(DC):
                        last = nc.scalar.activation(o_t[:, dc, :], misc[:, dc * 2 * P:(dc + 1) * 2 * P],
                                                    ACT.Identity, bias=v_bias[:, dc:dc + 1])
                    last.then_inc(misc_free, 1)
                elif what == "mtr":
                    wait(eng, max_in[hg], lin(b, MAX_IN, MAX_IN))
                    nc.scalar.activation(max_t[:, :], misc16[0:HG * MROWS * TB, 0:P], ACT.Copy)\
                        .then_inc(misc_free, 1)

            def handle(b, n, hg, kind, *a):
                if kind == "st":
                    g, h = a
                    u = HG * g + h
                    off = group_shape(g)[2]
                    if h == 0:
                        wait(eng, pv_done, lin(b, NGRP * NG, NGRP * hg + g - 1))
                    eng.wait_ge(st_full, lin(b, NU * NG, NU * hg + u + 1))
                    nc.scalar.activation(probs[:, g % 2, h, 0:CW - off], st_bank[u % 3][:, 0:CW - off], ACT.Exp)\
                        .then_inc(exp_done, 1)
                elif kind == "oev":
                    c = a[0]
                    eng.wait_ge(pv_done, lin(b, NGRP * NG, NGRP * hg + (CT, 0)[c]))
                    nc.scalar.activation(o_raw[:, c * CW:(c + 1) * CW], o_bank[:, :], ACT.Copy).then_inc(o_out, 1)
                elif kind == "use":
                    evict(b, n, hg, *a)

            moe_scalar(0)
            eng.wait_ge(bias_scaled, 1)
            walk(eng, handle)
            moe_scalar(1)

        @block.vector
        def _(eng):
            for bank in st_bank + s_bank + [o_bank, misc]:
                nc.vector.memset(bank[:, :], 0.0)
            eng.drain().then_inc(consts_ready, 1)

            def gate_round(slot, chunk):
                odd = slot % 2
                if 0 in chunk:
                    c = chunk[0]
                    eng.wait_ge(x_in[slot], (c - slot) * (16 // LOADS) + 16)
                    wait(eng, stats_ready, c)
                    for t in range(CT):
                        vector_stats(t, c * CT + t)
                if 1 in chunk:
                    c = chunk[1]
                    eng.wait_ge(rstd_ready, c + 1)
                    wait(eng, gate_xt_full, c * 2 - 2)
                    for t in range(CT):
                        vector_normalise(t, c * CT + t, gate_xn[1 - odd]).then_inc(xn_ready, 1)
                if 0 in chunk:
                    vector_aggregate(eng).then_inc(stats_ready, 1)

            gate_pipeline(eng, 2, gate_round)

            def top2_and_counts(layer, logits_in, value):
                eng.wait_ge(logits_in, value)
                vec = nc.vector
                wide = lambda ap: ap.to_broadcast([P, NT, E])
                eng.drain()
                vec.tensor_copy(left, logits[:, :, :])
                for choice in range(2):
                    eng.drain()
                    vec.tensor_reduce(top[:, :, 0], left, AX.X, ALU.max)
                    eng.drain()
                    vec.tensor_tensor(work, left, wide(top[:, :, :]), ALU.is_equal)
                    eng.drain()
                    vec.tensor_tensor(work, work, wide(rank[:, :, :]), ALU.mult)
                    eng.drain()
                    vec.tensor_reduce(best[:, :, 0], work, AX.X, ALU.max)
                    eng.drain()
                    vec.tensor_tensor(work, work, wide(best[:, :, :]), ALU.is_equal)
                    eng.drain()
                    if choice == 0:
                        vec.tensor_copy(chosen, work)
                        vec.scalar_tensor_tensor(out=left, in0=work, scalar=-BIG, in1=left, op0=ALU.mult,
                                                 op1=ALU.add)
                    else:
                        vec.tensor_tensor(chosen, chosen, work, ALU.add)
                eng.drain()
                vec.tensor_reduce(counts[:, :], chosen.rearrange("p t e -> p e t"), AX.X, ALU.add)\
                    .then_inc(counted, 1)
                if layer == 0:
                    eng.wait_ge(weights_in, 16 * WEIGHT_DMAS)
                    nc.vector.tensor_scalar(qk_bias[0:HG * HD, :], qk_bias[0:HG * HD, :], HD ** -0.5, None,
                                            ALU.mult).then_inc(bias_scaled, 1)
                eng.wait_ge(totalled, layer + 1)
                vec.tensor_scalar(kept[:, 0, :], total[:, :], float(CAP), None, ALU.is_le)
                eng.drain()
                vec.tensor_reduce(any_kept[:, :], kept[:, 0, :], AX.X, ALU.max)
                eng.drain()
                vec.tensor_copy(flag[:, :], any_kept[:, :]).then_inc(flag_ready, 1)

            def moe_vector(layer):
                vec = nc.vector
                wide = lambda ap: ap.to_broadcast([P, NT, E])

                def gate():
                    vec.tensor_reduce(top[:, :, 0], logits[:, :, :], AX.X, ALU.max)
                    eng.drain()
                    vec.tensor_tensor(left, logits[:, :, :], wide(top[:, :, :]), ALU.subtract)\
                        .then_inc(baton[layer], 1)
                    eng.wait_ge(baton[layer], 2)
                    vec.tensor_reduce(top[:, :, 0], work, AX.X, ALU.add)
                    eng.drain()
                    vec.reciprocal(best[:, :, :], top[:, :, :])
                    eng.drain()
                    vec.tensor_tensor(work, work, wide(best[:, :, :]), ALU.mult)
                    eng.drain()
                    vec.tensor_tensor(work, work, chosen, ALU.mult)
                    eng.drain()
                    vec.tensor_tensor(work, work, wide(kept[:, :, :]), ALU.mult)
                    eng.drain()
                    vec.tensor_scalar(work, work, 0.5, None, ALU.mult).then_inc(baton[layer], 1)

                def chunk(c, i, turn):
                    eng.wait_ge(baton[layer], turn(0))
                    for t in range(CT):
                        vector_stats(t, c * CT + t)
                    vector_aggregate(eng).then_inc(baton[layer], 1)
                    eng.wait_ge(baton[layer], turn(2))
                    for t in range(CT):
                        last = vector_normalise(t, c * CT + t)
                    last.then_inc(baton[layer], 1)

                weight = probs[:, 0, 1, :]

                def expert(c, e):
                    eng.wait_ge(baton[layer], moe_value(c, e, 2))
                    vec.tensor_scalar(hidden_e, hidden_e, 1.0, None, ALU.add)
                    eng.drain()
                    vec.reciprocal(hidden_e, hidden_e)
                    eng.drain()
                    vec.tensor_tensor(hidden, hidden, hidden_e, ALU.mult).then_inc(baton[layer], 1)
                    eng.wait_ge(baton[layer], moe_value(c, e, 4))
                    for j in range(2):
                        vec.tensor_tensor(y_e[:, 2 * j:2 * j + 2, :],
                                          s_bank[j][:, :].rearrange("p (t d) -> p t d", t=2),
                                          b2_e.to_broadcast([P, 2, D]), ALU.add)
                    eng.drain()
                    for t in range(CT):
                        tile = x_tiles(c * CT + t, 1)[:, 0, :]
                        last = vec.scalar_tensor_tensor(out=tile, in0=y_e[:, t, :],
                                                        scalar=weight[:, bass.ds(c * (CT * E) + e + t * E, 1)],
                                                        in1=tile, op0=ALU.mult, op1=ALU.add)
                    last.then_inc(baton[layer], 1)

                moe_experts(eng, layer, gate, chunk, expert)

            def handle(b, n, hg, kind, *a):
                if kind == "s":
                    ahead, u = a
                    ib, h, j0, width, diag = MAX_UNITS[u]
                    eng.wait_ge(s_full, lin(b, NU * NG, NU * (hg + ahead) + u + 1))
                    if diag:
                        passed(eng, "vector")
                    bank = s_bank[u % 3][:, 0:width]
                    if diag:
                        nc.vector.tensor_tensor_reduce(out=bank, in0=bank, in1=causal[:, CW - width:CW],
                                                       scale=1.0, scalar=-BIG, op0=ALU.add, op1=ALU.max,
                                                       accum_out=max_diag[:, h, ib:ib + 1]).then_inc(max_done, 1)
                    else:
                        nc.vector.tensor_reduce(max_full[:, h, ib - CT:ib - CT + 1], bank, AX.X, ALU.max)\
                            .then_inc(max_done, 1)
                elif kind == "mfin":
                    eng.drain()
                    late = max_diag[:, :, CT:TB]
                    nc.vector.tensor_tensor(late, late, max_full[:, :, :], ALU.max)
                    eng.drain()
                    nc.vector.tensor_scalar(max_parts[:, 0, :, :], max_diag[:, :, :], -1.0, None, ALU.mult)
                    eng.drain()
                    nc.vector.scalar_tensor_tensor(out=max_rest[:, :, :], in0=max_diag[:, :, :], scalar=-1.0,
                                                   in1=max_parts[:, 0, :, :], op0=ALU.mult, op1=ALU.subtract)
                    eng.drain()
                    nc.vector.tensor_copy(max_parts[:, 1, :, :], max_rest[:, :, :])
                    eng.drain()
                    nc.vector.tensor_tensor(max_parts[:, 2, :, :], max_rest[:, :, :], max_parts[:, 1, :, :],
                                            ALU.subtract).then_inc(mparts_ready, 1)
                elif kind in ("lnstat", "lnnorm"):
                    what, c, t = a
                    tile = lin(b, TB, (TB if what == "x" else -TB) + c * CT + t)
                    if kind == "lnstat":
                        if t == 0:
                            eng.drain()
                        vector_stats(t, tile)
                    else:
                        if t == 0:
                            eng.wait_ge(rstd_ready, n("lnaggr"))
                            eng.wait_ge(misc_full, n("use"))
                        vector_normalise(t, tile).then_inc(xn_ready, 1)
                elif kind == "lnaggr":
                    vector_aggregate(eng).then_inc(stats_ready, 1)
                elif kind == "q2":
                    hq, c = a
                    m = hq if hg == 0 else hq + NG
                    eng.wait_ge(rest_ready, lin(b, 2 * NG, 2 * m + c + 1))
                    nc.vector.tensor_copy(parts[:, c, 1, :], rest[:, :]).then_inc(part2_ready, 1)
                elif kind == "use" and a[0] == "otr":
                    hq, c = a[1:]
                    eng.wait_ge(misc_full, n("use", 1))
                    heads = misc[:, :].rearrange("p (q w) -> p q w", w=32)
                    nc.vector.reciprocal(sum_inv[:, :, :], heads[:, :, HD:VW])
                    eng.drain()
                    nc.vector.tensor_tensor(
                        o_tok[:, c * CT:(c + 1) * CT, hq * HG * HD:(hq + 1) * HG * HD]
                        .rearrange("p t (h d) -> p t h d", h=HG),
                        heads[:, :, 0:HD].rearrange("p (t h) d -> p t h d", t=CT),
                        sum_inv[:, :, :].to_broadcast([P, CT * HG, HD])
                        .rearrange("p (t h) d -> p t h d", t=CT), ALU.mult).then_inc(misc_free, 1)
                elif kind == "use" and a[0] == "wo":
                    j = a[1]
                    eng.wait_ge(misc_full, n("use", 1))
                    eng.wait_ge(bo_added, lin(b, 4, j + 1 - 4))
                    now = x_tiles(b * TB + (2 * j - TB), 2)
                    nc.vector.tensor_tensor(now, misc[:, :].rearrange("p (t d) -> p t d", t=2), now, ALU.add)\
                        .then_inc(misc_free, 1)

            top2_and_counts(0, gate_lt_taken, NCH)
            moe_vector(0)
            walk(eng, handle)
            top2_and_counts(1, misc_free, COUNTS_AFTER["use"] + 1)
            moe_vector(1)

        @block.tensor
        def _(eng):
            eng.wait_ge(consts_ready, CONSTS)
            eng.wait_ge(gate_weight_in, 16)
            def gate_round(slot, chunk):
                odd = slot % 2
                if 0 in chunk:
                    eng.wait_ge(xn_ready, chunk[0] * CT + CT)
                    for j in range(2):
                        wait(eng, gate_xt_taken, chunk[0] * 2 + (j - 3))
                        tensor_transpose_tiles(gate_bank[odd][j], gate_xn[odd], 2 * j).then_inc(gate_xt_full, 1)
                if 1 in chunk:
                    eng.wait_ge(gate_xt_taken, chunk[1] * 2 + 2)
                    wait(eng, gate_lg_taken, chunk[1] - 1)
                    tensor_gate_logits(gate_bank[1 - odd][2], gate_xt_of(chunk[1], 1 - odd)).then_inc(gate_lg_full, 1)
                if 2 in chunk:
                    eng.wait_ge(gate_lg_taken, chunk[2] + 1)
                    wait(eng, gate_lt_taken, chunk[2] - 1)
                    nc.tensor.transpose(gate_bank[odd][3][:, 0:P], gate_lg[odd], ident[:, :])\
                        .then_inc(gate_lt_full, 1)

            gate_pipeline(eng, 3, gate_round)

            def moe_tensor(layer):
                def chunk(c, i, turn):
                    eng.wait_ge(baton[layer], turn(3))
                    for t in range(CT):
                        for dc in range(DC):
                            last = nc.tensor.transpose(st_bank[dc][:, t * P:(t + 1) * P],
                                                       xn[:, t, dc * P:(dc + 1) * P], ident[:, :])
                    last.then_inc(baton[layer], 1)

                def expert(c, e):
                    eng.wait_ge(baton[layer], moe_value(c, e, 0))
                    eng.wait_ge(moe_weights_in[layer], c * (64 * E) + e * 64 + 64)
                    for fc in range(DC):
                        for dc in range(DC):
                            last = nc.tensor.matmul(st_bank[fc][:, :], w1_e[:, dc, fc * P:(fc + 1) * P],
                                                    xg_t[:, dc, :], start=dc == 0, stop=dc == DC - 1)
                    last.then_inc(baton[layer], 1)
                    eng.wait_ge(baton[layer], moe_value(c, e, 3))
                    for t in range(CT):
                        for fc in range(DC):
                            last = nc.tensor.matmul(s_bank[t // 2][:, t % 2 * D:(t % 2 + 1) * D],
                                                    hidden[:, fc, t * P:(t + 1) * P], w2_e[:, fc, :],
                                                    start=fc == 0, stop=fc == DC - 1)
                    last.then_inc(baton[layer], 1)

                moe_experts(eng, layer, None, chunk, expert)

            def fill(b, n, hg, what, *a):
                wait(eng, misc_free, n("use", 1))
                if what == "v":
                    for t in range(2):
                        for dc in range(DC):
                            t0 = (2 * a[0] + t) * P
                            last = nc.tensor.matmul(misc[:, t * D:(t + 1) * D], x_t[:, dc, t0:t0 + P],
                                                    w_v[:, dc, :], start=dc == 0, stop=dc == DC - 1)
                elif what == "qk":
                    hq, c = a
                    for dc in range(DC):
                        last = nc.tensor.matmul(misc[:, :], w_qk[:, dc, hq, :], x_t[:, dc, c * CW:(c + 1) * CW],
                                                start=dc == 0, stop=dc == DC - 1)
                elif what in ("xt", "xg"):
                    eng.wait_ge(xn_ready, n("lnnorm"))
                    last = tensor_transpose_tiles(misc, xn, 2 * a[1])
                elif what == "lg":
                    last = tensor_gate_logits(misc, xg_t)
                elif what == "lt":
                    last = nc.tensor.transpose(misc[:, 0:P], lg_t[:, :], ident[:, :])
                elif what == "otr":
                    c = a[1]
                    eng.wait_ge(o_out, lin(b, 2 * NG, 2 * hg + c - 1))
                    for t in range(CT):
                        t0 = c * CW + t * P
                        last = nc.tensor.transpose(misc[:, t * P:(t + 1) * P], o_raw[:, t0:t0 + P], ident[:, :])
                elif what == "ont":
                    last = tensor_transpose_tiles(misc, o_tok, 2 * a[0])
                elif what == "wo":
                    for t in range(2):
                        for dc in range(DC):
                            last = nc.tensor.matmul(misc[:, t * D:(t + 1) * D], o_t[:, dc, t * P:(t + 1) * P],
                                                    w_o[:, dc, :], start=dc == 0, stop=dc == DC - 1)
                elif what == "mtr":
                    eng.wait_ge(mparts_ready, lin(b, NG, hg + 2))
                    last = nc.tensor.transpose(misc16[0:HG * MROWS * TB, 0:P],
                                               max_parts[:, :, :, :].rearrange("p k h t -> p (k h t)"),
                                               ident16[:, :])
                last.then_inc(misc_full, 1)

            def handle(b, n, hg, kind, *a):
                if kind == "st":
                    g, h = a
                    qc, jb, off, _ = group_shape(g)
                    u = HG * g + h
                    if u == 0:
                        eng.wait_ge(stack_in[hg], lin(b, STACK_IN, STACK_IN))
                        eng.wait_ge(max_in[hg], lin(b, MAX_IN, MAX_IN))
                    wait(eng, exp_done, lin(b, NU * NG, NU * hg + u - 2))
                    nc.tensor.matmul(st_bank[u % 3][:, 0:CW - off],
                                     k_stack[0:KROWS + MROWS, hg, h, jb * P:(jb + 1) * P],
                                     q_stack[0:KROWS + MROWS, hg, h, qc * CW + off:(qc + 1) * CW],
                                     start=True, stop=True).then_inc(st_full, 1)
                elif kind == "s":
                    ahead, u = a
                    hm = (hg + ahead) % NG
                    ib, h, j0, width, _ = MAX_UNITS[u]
                    if u == 0:
                        eng.wait_ge(stack_in[hm], lin(b, STACK_IN, STACK_IN * (1 + (hg + ahead) // NG)))
                    wait(eng, max_done, lin(b, NU * NG, NU * (hg + ahead) + u - 2))
                    nc.tensor.matmul(s_bank[u % 3][:, 0:width], q_stack[0:KROWS, hm, h, ib * P:(ib + 1) * P],
                                     k_stack[0:KROWS, hm, h, j0:j0 + width], start=True, stop=True)\
                        .then_inc(s_full, 1)
                elif kind == "pv":
                    g = a[0]
                    back = g >= NGRP - 2
                    of = hg - back
                    _, jb, off, diag = group_shape(g)
                    if g == 0:
                        wait(eng, o_out, lin(b, 2 * NG, 2 * hg))
                    if g == CT:
                        eng.wait_ge(o_out, lin(b, 2 * NG, 2 * hg + 1))
                    if hg == 0 and not back and jb % 2 == 0 and diag:
                        eng.wait_ge(misc_free, n("use", 1))
                    if diag:
                        eng.wait_ge(sel_done, lin(b, 8 * NG, 8 * of + (g if g < CT else g - CT) + 1))
                    else:
                        eng.wait_ge(exp_done, lin(b, NU * NG, NU * of + HG * g + HG))
                    for h in range(HG):
                        last = nc.tensor.matmul(o_bank[32 * h:32 * h + VW, off:CW],
                                                v_aug[:, jb, of % NG * HG + h, :],
                                                probs[:, g % 2, h, 0:CW - off], start=g in (0, CT),
                                                stop=g in (CT - 1, NGRP - 1))
                    last.then_inc(pv_done, 1)
                elif kind == "use":
                    fill(b, n, hg, *a)

            moe_tensor(0)
            eng.wait_ge(weights_in, 16 * WEIGHT_DMAS)
            walk(eng, handle)
            moe_tensor(1)


_OUT_SHAPE = (NT, P, D)


def kernel(L0_attn_x, L0_attn_Wq, L0_attn_bq, L0_attn_Wkv, L0_attn_bkv, L0_attn_Wo, L0_attn_bo,
           L0_ffn_gate_w, L0_ffn_w1, L0_ffn_b1, L0_ffn_w2, L0_ffn_b2):
    import numpy as np
    import concourse.bacc as bacc
    from concourse.bass_utils import run_bass_kernel_spmd

    def grouped(q, k):
        parts = [p.reshape(p.shape[:-1] + (NG, HG, HD)).swapaxes(-1, -2).reshape(p.shape[:-1] + (NG, HG * HD))
                 for p in (q, k)]
        return np.concatenate(parts, axis=-1)

    a = {n: np.asarray(v) for n, v in locals().items() if n.startswith("L0_")}
    wk, wv = a["L0_attn_Wkv"][:D], a["L0_attn_Wkv"][D:]
    arrays = {
        "x": a["L0_attn_x"].reshape(_OUT_SHAPE),
        "wqk_t": grouped(a["L0_attn_Wq"].T, wk.T),
        "wv_t": wv.T,
        "wo_t": a["L0_attn_Wo"].T,
        "bqk": grouped(a["L0_attn_bq"], a["L0_attn_bkv"][:D]),
        "bv": a["L0_attn_bkv"][D:],
        "bo": a["L0_attn_bo"],
        "gate_t": a["L0_ffn_gate_w"].T,
        "w1_t": a["L0_ffn_w1"].transpose(0, 2, 1),
        "b1": a["L0_ffn_b1"],
        "w2_t": a["L0_ffn_w2"].transpose(0, 2, 1),
        "b2": a["L0_ffn_b2"],
    }
    arrays = {n: np.ascontiguousarray(v) for n, v in arrays.items()}
    nc = bacc.Bacc("TRN2", target_bir_lowering=False, num_devices=1)
    nc.disable_value_cache = True
    args = [nc.dram_tensor(n, v.shape, mybir.dt.from_np(v.dtype), kind="ExternalInput").ap()
            for n, v in arrays.items()]
    out = nc.dram_tensor("out", _OUT_SHAPE, FP32, kind="ExternalOutput").ap()
    program(nc, *args, out)
    r = run_bass_kernel_spmd(nc, [arrays], core_ids=[0])
    return r.results[0]["out"].reshape(B, S, D)
```

```python
import struct

import concourse.bass as bass
from concourse import mybir
from contextlib import ExitStack

FP32 = mybir.dt.float32
BF16 = mybir.dt.bfloat16
INT32 = mybir.dt.int32
ALU = mybir.AluOpType
ACT = mybir.ActivationFunctionType
AX = mybir.AxisListType
ADD_REDUCE = bass.bass_isa.ReduceOp.add

B, S, D = 8, 1024, 256
H, HD = 16, 16
HG, NG = 4, 4
P = 128
TB = S // P
NT = B * TB
DC = D // P
CW = 512
CT = CW // P
NCH = B * S // CW
TOP2_EARLY = (B - 1) * TB - CT
LOADS = 4
E = 8
CAP = int(1.25 * B * S / E)
EPS = 1e-5
KROWS = 6 * HD
MROWS = 3
VW = HD + 1
BIG = 3.0e38
TWO_ONES = struct.unpack("<f", struct.pack("<I", 0x3F803F80))[0]
NU = 48
NGRP = NU // HG
RUNS = ((0, 3, 0), (3, 2, 1), (5, 1, 2))
STACK_DMAS = 2 * len(RUNS)


PLACE = {
    "v": (5, 9, 18, 21), "otr3": (1, 12), "qk3": (15, 24), "x_norm": (8, 24), "xt": (27, 30, 38, 44),
    "bo": (8, 20, 28, 36), "ont": (1, 10, 20, 30), "wo": (7, 16, 25, 36), "otr0": (13, 33), "qk0": (4, 23),
    "otr1": (0, 9), "qk1": (5, 26), "gate0": (4, 19, 23, 31, 43),
    "otr2": (1, 9), "qk2": (5, 22), "gate1": (4, 18, 26, 31, 37),
    "end": (24, 26, 29, 32, 35), "top2": 17,
    "mtr": (8, 7, 5, 7),
}
PROLOGUE_FIRST, PROLOGUE_STEP = 2, 9
NORM_STEP = 1
NORM_LAG = 9
Q2_LAG, Q3_LAG = 3, 5
MFIN_PARTS = 5
OEV_AT = 0
EARLY = 15


def group_shape(g):
    if g < CT:
        return 0, g, g * P, True
    jb = g - CT
    return 1, jb, max(0, jb - CT) * P, jb >= CT


def max_units():
    full = [(ib, h, 0, CW, False) for ib in range(CT, TB) for h in range(HG)]
    diag = [(ib, h, ib // CT * CW, (ib % CT + 1) * P, True) for ib in range(TB) for h in range(HG)]
    out = []
    for i, f in enumerate(full):
        out += [f, diag[2 * i], diag[2 * i + 1]]
    return out


MAX_UNITS = max_units()


def step_plan(hg, prev, nxt):
    extra = {}

    def put(u, *events):
        extra.setdefault(u, []).extend(events)

    def norm_jobs(kind, c, u):
        for t in range(CT):
            put(u + NORM_STEP * t, ("lnstat", kind, c, t))
            put(u + NORM_LAG + NORM_STEP * t, ("lnnorm", kind, c, t))
        put(u + NORM_STEP * CT - NORM_STEP + 1, ("lnaggr", kind, c))

    def project():
        hq = (hg + NG - 1) % NG
        for c, u in enumerate(PLACE[f"qk{hq}"]):
            put(u, ("use", "qk", hq, c))
            put(u + Q2_LAG, ("q2", hq, c))
            put(u + Q3_LAG, ("q3", hq, c))

    def heads_out():
        hq = (hg + NG - 1) % NG
        for c, u in enumerate(PLACE[f"otr{hq}"]):
            put(u, ("use", "otr", hq, c))

    def gate_jobs(c):
        norm, *units = PLACE[f"gate{c}"]
        norm_jobs("last", c, norm)
        for u, job in zip(units, (("xg", c, 0), ("xg", c, 1), ("lg", c), ("lt", c, "last"))):
            put(u, ("use",) + job)

    if hg > 0 or prev:
        heads_out()
    if prev if hg == 0 else nxt:
        project()
    if hg == 0:
        if prev:
            for j, u in enumerate(PLACE["v"]):
                put(u, ("use", "v", j))
        if nxt:
            for c, u in enumerate(PLACE["x_norm"]):
                norm_jobs("next", c, u)
            for i, u in enumerate(PLACE["xt"]):
                put(u, ("use", "xt", i // 2, i % 2))
    if hg == 1:
        for i, u in enumerate(PLACE["bo"]):
            put(u, ("bo", i))
        if prev:
            for j in range(4):
                put(PLACE["ont"][j], ("use", "ont", j))
                put(PLACE["wo"][j], ("use", "wo", j, "last"))
            put(PLACE["wo"][-1] + 2, ("out",))
    if hg >= 2 and prev:
        gate_jobs(hg - 2)
    if hg == NG - 1 and not nxt:
        for u, job in zip(PLACE["end"], (("otr", 3, 0), ("ont", 0), ("wo", 0, "this"), ("ont", 1),
                                                 ("wo", 1, "this"))):
            put(u, ("use",) + job)
        norm_jobs("this", 0, NU - 1 - NORM_LAG - NORM_STEP * (CT - 1))
        put(PLACE["top2"], ("top2",))
    if hg < NG - 1 or nxt:
        for k in range(MFIN_PARTS):
            put(NU - EARLY + k, ("mfin", k))
        put(NU - EARLY + PLACE["mtr"][hg], ("use", "mtr"), ("mdma",))
    plan = []
    for g in range(NGRP):
        for h in range(HG):
            plan.append(("st", g, h))
            if h == 0 and not (hg == 0 and not prev and g < 2):
                plan.append(("pv", (g - 2) % NGRP))
            if h == OEV_AT and g in (1, CT + 1) and not (hg == 0 and not prev and g == 1):
                plan.append(("oev", int(g == 1)))
            u = HG * g + h + EARLY
            ahead = 1 + u // NU
            if hg + ahead < NG or nxt:
                plan.append(("s", ahead, u % NU))
            plan += extra.get(HG * g + h, [])
    return [(hg,) + e for e in plan]


def batch_plan(prev, nxt):
    return [e for hg in range(NG) for e in step_plan(hg, prev, nxt)]


def prologue_plan():
    def project(hq, c):
        return [(3, "use", "qk", hq, c), (3, "q2", hq, c), (3, "q3", hq, c)]

    plan = project(0, 0) + project(0, 1) + [(3, "use", "v", j) for j in range(4)]
    halves = [(hq, c) for hq in range(1, NG) for c in range(2)]
    for u in range(NU + EARLY):
        if u == NU:
            plan += [(3, "mfin", k) for k in range(MFIN_PARTS)]
        plan.append((3, "s", 1 + u // NU, u % NU))
        for i, half in enumerate(halves):
            first = PROLOGUE_FIRST + i * PROLOGUE_STEP
            plan += [job for job, at in zip(project(*half), (first, first + 7, first + 9)) if at == u]
        if u == NU + 2:
            plan += [(3, "use", "mtr"), (3, "mdma",)]
    return plan


def epilogue_plan():
    def use(*a):
        return (0, "use") + a

    def norm(c):
        return ([(0, "lnstat", "last", c, t) for t in range(CT)] + [(0, "lnaggr", "last", c)]
                + [(0, "lnnorm", "last", c, t) for t in range(CT)])

    plan = [(0, "pv", NGRP - 2), (0, "pv", NGRP - 1), (0, "oev", 1), use("xg", 0, 0), use("xg", 0, 1),
            use("otr", 3, 1), use("ont", 2), use("lg", 0), use("wo", 2, "last"), use("ont", 3),
            use("lt", 0, "last"), use("wo", 3, "last"), (0, "out")]
    return plan + norm(1) + [use("xg", 1, 0), use("xg", 1, 1), use("lg", 1), use("lt", 1, "last")]


BATCH = {"last": -1, "this": 0, "next": 1}


def count(plan, kind):
    return sum(e[1] == kind for e in plan)


def make_sections():
    before = {"use": 0, "lnaggr": NCH, "lnnorm": CT * NCH}
    out = []
    for plan, times, b in ((prologue_plan(), 1, -1), (batch_plan(False, True), 1, 0),
                           (batch_plan(True, True), B - 2, 1), (batch_plan(True, False), 1, B - 1),
                           (epilogue_plan(), 1, B)):
        out.append((plan, times, b, dict(before)))
        for k in before:
            before[k] += times * count(plan, k)
    return out, before


SECTIONS, COUNTS_AFTER = make_sections()


def walk(eng, handle):
    for plan, times, b0, start in SECTIONS:
        def events(b):
            seen = dict.fromkeys(start, 0)
            for hg, kind, *a in plan:
                def n(k, more=0):
                    if times == 1:
                        return start[k] + seen[k] + more
                    per = count(plan, k)
                    return b * per + (start[k] + seen[k] + more - per * b0)
                handle(b, n, hg, kind, *a)
                if kind in seen:
                    seen[kind] += 1
        if times == 1:
            events(b0)
        else:
            with eng.Fori(b0, b0 + times) as b:
                events(b)


def wait(eng, sem, value):
    if not isinstance(value, int) or value > 0:
        eng.wait_ge(sem, value)


def program(nc, x, wqk_t, wv_t, wo_t, bqk, bv, bo, gate_t, w1_t, b1, w2_t, b2, out):
    with ExitStack() as ctx:
        ctx.enter_context(nc.allow_non_contiguous_dma(reason="biases and gate columns"))

        def sb(name, shape, dt=FP32):
            return ctx.enter_context(nc.sbuf_tensor(name, shape, dt))

        def pb(name):
            return ctx.enter_context(nc.psum_tensor(name, [P, CW], FP32))

        def sem(name):
            return ctx.enter_context(nc.semaphore(name))

        x_all = sb("x_all", [P, NT, D])
        w_qk = sb("w_qk", [P, DC, NG, P])
        w_v = sb("w_v", [P, DC, D])
        w_o = sb("w_o", [P, DC, D])
        w_gate = sb("w_gate", [P, DC, 32])
        qk_bias = sb("qk_bias", [P, NG])
        qk_scale = sb("qk_scale", [P, 1])
        v_bias = sb("v_bias", [P, DC])
        bo_row = sb("bo_row", [P, 1, D])
        ident = sb("ident", [P, P])
        ident16 = sb("ident16", [P, P], BF16)
        causal = sb("causal", [P, CW], BF16)
        neg_half = sb("neg_half", [P, CT])
        stats = sb("stats", [P, CT, 6])
        mean_var = sb("mean_var", [P, CT, 2])
        rstd = sb("rstd", [P, CT])
        xn = sb("xn", [P, CT, D])
        x_t = sb("x_t", [P, DC, S])
        xg_t = sb("xg_t", [P, DC, CW])
        qk32 = sb("qk32", [P, CW])
        rest = sb("rest", [P, CW])
        parts = sb("parts", [P, 2, 3, CW], BF16)
        q_stack = sb("q_stack", [P, NG, HG, S], BF16)
        k_stack = sb("k_stack", [P, NG, HG, S], BF16)
        v_aug = sb("v_aug", [P, TB, H, VW])
        probs = sb("probs", [P, 2, HG, CW])
        o_raw = sb("o_raw", [P, S])
        sum_inv = sb("sum_inv", [P, CT * HG, 1])
        o_tok = sb("o_tok", [P, TB, D])
        o_t = sb("o_t", [P, DC, 2 * P])
        max_diag = sb("max_diag", [P, 2, HG, TB])
        max_full = sb("max_full", [P, 2, HG, CT])
        max_rest = sb("max_rest", [P, HG, TB])
        max_parts = sb("max_parts", [P, MROWS, HG, TB], BF16)
        max_t = sb("max_t", [HG * MROWS * TB, P], BF16)
        lg_t = sb("lg_t", [P, P])
        logits = sb("logits", [P, NT, E])
        rank = sb("rank", [P, 1, E])
        counts = sb("counts", [P, E])
        total = sb("total", [P, E])
        kept = sb("kept", [P, 1, E])
        any_kept = sb("any_kept", [P, 1])
        flag = sb("flag", [P, 1], INT32)
        def gate_tables(wide, narrow):
            return ([w[:, 0:NT * E].rearrange("p (t e) -> p t e", e=E) for w in wide]
                    + [narrow[:, i * NT:(i + 1) * NT].rearrange("p (t e) -> p t e", e=1) for i in range(2)])

        tables = (gate_tables([probs[:, 0, i, :] for i in range(3)], probs[:, 0, 3, :]),
                  gate_tables([x_t[:, 0, 0:CW], x_t[:, 0, CW:S], x_t[:, 1, 0:CW]], x_t[:, 1, CW:S]))
        gate_xn = (xn[:, :, :], probs[:, 1, 0:2, :].rearrange("p a (t d) -> p (a t) d", d=D))
        gate_xt = (xg_t[:, :, :], o_tok[:, :, :].rearrange("p (c t) d -> p c (t d)", c=DC)[:, :, 0:CW])
        gate_lg = (lg_t[:, :], rest[:, 0:P])
        moe_space = q_stack[:, :, :, :].rearrange("p g h s -> p (g h s)").bitcast(FP32)
        w1_e = moe_space[:, 0:512].rearrange("p (c f) -> p c f", c=DC)
        w2_e = moe_space[:, 512:1024].rearrange("p (c f) -> p c f", c=DC)
        b2_e = moe_space[:, 1024:1280].rearrange("p (t f) -> p t f", t=1)
        b1_e = moe_space[:, 1280:1282]
        hidden = moe_space[:, 2048:3072].rearrange("p (c t) -> p c t", c=DC)
        hidden_e = moe_space[:, 3072:4096].rearrange("p (c t) -> p c t", c=DC)
        y_e = moe_space[:, 4096:5120].rearrange("p (t f) -> p t f", t=CT)

        st_bank = [pb(f"st{i}") for i in range(3)]
        s_bank = [pb(f"s{i}") for i in range(3)]
        o_bank = pb("o_bank")
        misc = pb("misc")
        misc16 = misc[:, :].bitcast(BF16)
        gate_bank = ((*st_bank, s_bank[0]), (s_bank[1], s_bank[2], o_bank, misc))

        part_dram = nc.dram_tensor("part_dram", [NG, 2, 3, HG * HD, S], BF16, kind="Internal").ap()

        weights_in = sem("weights_in")
        gate_weight_in = sem("gate_weight_in")
        bias_scaled = sem("bias_scaled")
        consts_ready = sem("consts_ready")
        consts_step = sem("consts_step")
        x_in = [sem(f"x_in{i}") for i in range(LOADS)]
        misc_full = sem("misc_full")
        misc_free = sem("misc_free")
        stats_ready = sem("stats_ready")
        rstd_ready = sem("rstd_ready")
        xn_ready = sem("xn_ready")
        rest_ready = sem("rest_ready")
        part2_ready = sem("part2_ready")
        part3_ready = sem("part3_ready")
        parts_out = [sem(f"parts_out{i}") for i in range(2)]
        stack_in = [sem(f"stack_in{i}") for i in range(NG)]
        st_full = sem("st_full")
        exp_done = sem("exp_done")
        sel_done = sem("sel_done")
        pv_done = sem("pv_done")
        o_out = sem("o_out")
        s_full = sem("s_full")
        max_done = sem("max_done")
        mparts_ready = sem("mparts_ready")
        max_in = [sem(f"max_in{i}") for i in range(NG)]
        bo_added = sem("bo_added")
        out_written = sem("out_written")
        counted = sem("counted")
        totalled = sem("totalled")
        flag_ready = sem("flag_ready")
        baton = [sem(f"baton{i}") for i in range(2)]
        moe_weights_in = [sem(f"moe_weights_in{i}") for i in range(2)]

        wait_passed = {name: sem(f"wait_passed_{name}") for name in ("sync", "gpsimd", "vector")}

        WEIGHT_DMAS = 6
        CONSTS = 2
        STACK_IN, MAX_IN = 16 * STACK_DMAS, 16
        GATE_TURNS, CHUNK_TURNS, EXPERT_TURNS = 3, 5, 5
        TURNS = CHUNK_TURNS + E * EXPERT_TURNS

        def lin(b, k, c):
            return b * k + c

        def passed(eng, name):
            eng.sem_inc(wait_passed[name], 1)

        def x_tiles(t0, n):
            return x_all[:, bass.ds(t0, n), :]

        def row_out(t, width):
            return misc[:, t * width:(t + 1) * width]

        def vector_stats(t, tile):
            nc.vector.bn_stats(stats[:, t, :], x_tiles(tile, 1)[:, 0, :])

        def vector_aggregate(eng):
            eng.drain()
            for t in range(CT):
                last = nc.vector.bn_aggr(mean_var[:, t, :], stats[:, t, :])
            return last

        def vector_normalise(t, tile, dst=xn):
            return nc.vector.tensor_scalar(dst[:, t, :], x_tiles(tile, 1)[:, 0, :], mean_var[:, t, 0:1],
                                           rstd[:, t:t + 1], ALU.subtract, ALU.mult)

        def pool_rstd(eng, fenced, value):
            nc.gpsimd.tensor_scalar_add(rstd[:, :], mean_var[:, :, 1], EPS).then_inc(fenced, 1)
            eng.wait_ge(fenced, value)
            return nc.gpsimd.tensor_tensor(rstd[:, :], rstd[:, :], neg_half[:, :], ALU.pow)

        rstd_sum = sem("rstd_sum")
        gate_xt_full = sem("gate_xt_full")
        gate_xt_taken = sem("gate_xt_taken")
        gate_lg_full = sem("gate_lg_full")
        gate_lg_taken = sem("gate_lg_taken")
        gate_lt_full = sem("gate_lt_full")
        gate_lt_taken = sem("gate_lt_taken")

        def gate_xt_of(chunk, odd):
            if isinstance(chunk, int) and chunk < S // CW:
                return x_t[:, :, chunk * CW:(chunk + 1) * CW]
            return gate_xt[odd]

        def gate_pipeline(eng, stages, body):
            def peeled(i):
                body(i % LOADS, {k: i - k for k in range(stages) if 0 <= i - k < NCH})
            for i in range(LOADS):
                peeled(i)
            with eng.Fori(1, NCH // LOADS) as four:
                for slot in range(LOADS):
                    body(slot, {k: four * LOADS + (slot - k) for k in range(stages)})
            for i in range(NCH, NCH + stages - 1):
                peeled(i)

        moe_rstd_sum = [sem(f"moe_rstd_sum{i}") for i in range(2)]

        def tensor_gate_logits(bank, xt):
            for dc in range(DC):
                for t in range(CT):
                    last = nc.tensor.matmul(bank[32 * t:32 * t + 32, 0:P], w_gate[:, dc, :],
                                            xt[:, dc, t * P:(t + 1) * P], start=dc == 0, stop=dc == DC - 1)
            return last

        def tensor_transpose_tiles(dst, src, t0):
            for dc in range(DC):
                for t in range(2):
                    i = 2 * dc + t
                    last = nc.tensor.transpose(dst[:, i * P:(i + 1) * P],
                                               src[:, t0 + t, dc * P:(dc + 1) * P], ident[:, :])
            return last

        def pair_view(bank):
            return bank[:, :].rearrange("p (c t) -> p c t", c=DC)

        def logits_view(bank):
            return bank[:, 0:P].rearrange("p (t e) -> p t e", t=CT)[:, :, 0:E]

        def moe_value(c, e, turn):
            if e is None:
                return c * TURNS + (GATE_TURNS + turn)
            return c * TURNS + (e * EXPERT_TURNS + (GATE_TURNS + CHUNK_TURNS + turn))

        def moe_experts(eng, layer, gate, chunk, expert):
            eng.wait_ge(flag_ready, layer + 1)
            kept_here = eng.value_load(flag[0:1, 0:1], min_val=0, max_val=1)
            with eng.If(kept_here > 0):
                if gate:
                    gate()
                with eng.Fori(0, NCH) as c:
                    if chunk:
                        chunk(c, c, lambda turn: moe_value(c, None, turn))
                    with eng.Fori(0, E) as e:
                        expert(c, e)
                done = GATE_TURNS + NCH * TURNS
                if layer == 0:
                    for c in range(S // CW):
                        if chunk:
                            chunk(c, NCH + c, lambda turn: done + turn)
                        done += CHUNK_TURNS
                eng.wait_ge(baton[layer], done)
            with eng.Else():
                eng.nop()

        block = ctx.enter_context(nc.Block())

        @block.sync
        def _(eng):
            for k in range(LOADS):
                eng.dma_start(x_tiles(k * CT, CT), x[k * CT:(k + 1) * CT, :, :].rearrange("t p d -> p t d"))\
                   .then_inc(x_in[k], 16)
            with eng.Fori(1, NCH // LOADS) as i:
                for k in range(LOADS):
                    eng.wait_ge(x_in[k], i * 16)
                    passed(eng, "sync")
                    eng.dma_start(x_tiles(i * (LOADS * CT) + k * CT, CT),
                                  x[bass.ds(i * (LOADS * CT) + k * CT, CT), :, :].rearrange("t p d -> p t d"))\
                       .then_inc(x_in[k], 16)

            def moe_sync(layer):
                def expert(c, e):
                    eng.wait_ge(baton[layer], moe_value(c, e, 0))
                    passed(eng, "sync")
                    for dst, src in ((w1_e, w1_t[bass.ds(e, 1), :, :].rearrange("e (c p) f -> p (e c) f", p=P)),
                                     (w2_e, w2_t[bass.ds(e, 1), :, :].rearrange("e (c p) f -> p (e c) f", p=P)),
                                     (b1_e, b1[bass.ds(e, 1), :].rearrange("e (c p) -> p (e c)", p=P)),
                                     (b2_e, b2[bass.ds(e, 1), :].partition_broadcast(P))):
                        eng.dma_start(dst, src).then_inc(moe_weights_in[layer], 16)
                moe_experts(eng, layer, None, None, expert)

            def handle(b, n, hg, kind, *a):
                if kind == "q3":
                    hq, c = a
                    m = (4, hq if hg == 0 else hq + NG)
                    eng.wait_ge(part3_ready, lin(b, 2 * m[0], 2 * m[1] + c + 1))
                    passed(eng, "sync")
                    if c == 0:
                        wait(eng, stack_in[hq], lin(b, STACK_IN, 0 if hg == 0 else STACK_IN))
                    for qk in range(2):
                        eng.dma_start(part_dram[hq, qk, :, :, c * CW:(c + 1) * CW].rearrange("k p c -> p k c"),
                                      parts[qk * HG * HD:(qk + 1) * HG * HD, c, :, :]).then_inc(parts_out[c], 16)
                    if c == 1:
                        for half in range(2):
                            eng.wait_ge(parts_out[half], lin(b, 32 * m[0], 32 * m[1] + 32))
                            passed(eng, "sync")
                        wait(eng, pv_done, lin(b, NGRP * m[0], NGRP * (m[1] - 3)))
                        for r, times, part in RUNS:
                            rows = slice(r * HD, (r + times) * HD)
                            eng.dma_start(q_stack[rows, hq, :, :].rearrange("r h c -> r (h c)"),
                                          part_dram[hq, 0, 0:times, :, :].rearrange("k (d h) c -> (k d) (h c)", h=HG))\
                               .then_inc(stack_in[hq], 16)
                            eng.dma_start(k_stack[rows, hq, :, :].rearrange("r h c -> r (h c)"),
                                          part_dram[hq, 1, part, :, :].rearrange("(d h) c -> d (h c)", h=HG)
                                          .partition_broadcast(times)).then_inc(stack_in[hq], 16)
                elif kind == "mdma":
                    hm = (hg + 1) % NG
                    eng.wait_ge(misc_free, n("use", 1))
                    eng.dma_start(q_stack[KROWS:KROWS + MROWS, hm, :, :].rearrange("k h (t c) -> k (h t) c", c=P),
                                  max_t[:, :]).then_inc(max_in[hm], 16)
                elif kind == "out":
                    eng.wait_ge(misc_free, n("use", 1))
                    passed(eng, "sync")
                    eng.dma_start(out[bass.ds(b * TB - TB, TB), :, :].rearrange("t p d -> p t d"),
                                  x_tiles(b * TB - TB, TB)).then_inc(out_written, 16)

            moe_sync(0)
            walk(eng, handle)
            eng.wait_ge(out_written, 16 * B)
            moe_sync(1)
            with eng.If(eng.value_load(flag[0:1, 0:1], min_val=0, max_val=1) > 0):
                eng.dma_start(out.rearrange("t p d -> p t d"), x_all[:, :, :]).then_inc(out_written, 16)
                eng.wait_ge(out_written, 16 * B + 16)
            with eng.Else():
                eng.nop()

        @block.gpsimd
        def _(eng):
            nc.gpsimd.memset(ident[:, :], 0.0)
            nc.gpsimd.memset(causal[:, :], 0.0)
            nc.gpsimd.memset(w_gate[:, :, E:32], 0.0)
            nc.gpsimd.memset(neg_half[:, :], -0.5)
            nc.gpsimd.memset(qk_scale[:, :], 1.0).then_inc(consts_step, 1)
            eng.wait_ge(consts_step, 1)
            nc.gpsimd.affine_select(out=ident[:, :], in_=ident[:, :], compare_op=ALU.not_equal, fill=1.0,
                                    base=0, pattern=[[-1, P]], channel_multiplier=1)
            nc.gpsimd.affine_select(out=causal[:, CW - P:CW], in_=causal[:, CW - P:CW], compare_op=ALU.is_ge,
                                    fill=-BIG, base=0, pattern=[[-1, P]], channel_multiplier=1)
            nc.gpsimd.memset(qk_scale[0:HG * HD, :], HD ** -0.5)
            for e in range(E):
                nc.gpsimd.memset(rank[:, 0, e:e + 1], float(E - e))
            nc.gpsimd.memset(v_aug[:, :, :, HD:VW], 1.0).then_inc(consts_step, 1)
            eng.wait_ge(consts_step, 2)
            nc.gpsimd.tensor_copy(ident16[:, :], ident[:, :]).then_inc(consts_ready, 1)

            with eng.Fori(0, NCH) as c:
                eng.wait_ge(stats_ready, c + 1)
                passed(eng, "gpsimd")
                pool_rstd(eng, rstd_sum, c + 1).then_inc(rstd_ready, 1)

            def moe_pool(layer):
                eng.wait_ge(counted, layer + 1)
                nc.gpsimd.partition_all_reduce(total[:, :], counts[:, :], P, ADD_REDUCE).then_inc(totalled, 1)

                def chunk(c, i, turn):
                    eng.wait_ge(baton[layer], turn(1))
                    passed(eng, "gpsimd")
                    pool_rstd(eng, moe_rstd_sum[layer], i + 1).then_inc(baton[layer], 1)

                moe_experts(eng, layer, None, chunk, lambda c, e: eng.nop())

            def handle(b, n, hg, kind, *a):
                if kind == "st":
                    g, h = a
                    if h == HG - 1 and group_shape(g)[3]:
                        eng.wait_ge(exp_done, lin(b, NU * NG, NU * hg + HG * g + HG))
                        passed(eng, "gpsimd")
                        now = probs[:, g % 2, :, 0:P]
                        nc.gpsimd.affine_select(out=now, in_=now, compare_op=ALU.is_ge, fill=0.0, base=0,
                                                pattern=[[0, HG], [1, P]], channel_multiplier=-1)\
                            .then_inc(sel_done, 1)
                elif kind == "lnaggr":
                    eng.wait_ge(stats_ready, n("lnaggr", 1))
                    passed(eng, "gpsimd")
                    pool_rstd(eng, rstd_sum, n("lnaggr", 1)).then_inc(rstd_ready, 1)
                elif kind == "use" and a[0] == "qk":
                    hq, c = a[1:]
                    m = hq if hg == 0 else hq + NG
                    wait(eng, part3_ready, lin(b, 2 * NG, 2 * m + c))
                    eng.wait_ge(misc_free, n("use", 2))
                    nc.gpsimd.tensor_tensor(rest[:, :], qk32[:, :], parts[:, c, 0, :], ALU.subtract)\
                        .then_inc(rest_ready, 1)
                elif kind == "q3":
                    hq, c = a
                    m = hq if hg == 0 else hq + NG
                    eng.wait_ge(part2_ready, lin(b, 2 * NG, 2 * m + c + 1))
                    nc.gpsimd.tensor_tensor(parts[:, c, 2, :], rest[:, :], parts[:, c, 1, :], ALU.subtract)\
                        .then_inc(part3_ready, 1)
                elif kind == "bo":
                    eng.wait_ge(xn_ready, n("lnnorm"))
                    now = x_tiles(b * TB + 2 * a[0], 2)
                    nc.gpsimd.tensor_tensor(now, now, bo_row[:, :, :].to_broadcast([P, 2, D]), ALU.add)\
                        .then_inc(bo_added, 1)

            eng.wait_ge(rstd_ready, NCH)
            nc.gpsimd.memset(k_stack[P // 2:P, :, :, :].rearrange("p g h s -> p (g h s)").bitcast(FP32), TWO_ONES)\
                .then_inc(misc_free, 1)
            eng.wait_ge(weights_in, 16 * WEIGHT_DMAS)
            eng.wait_ge(misc_free, 1)
            moe_pool(0)
            walk(eng, handle)
            moe_pool(1)

        @block.scalar
        def _(eng):
            eng.dma_start(w_gate[:, :, 0:E], gate_t.rearrange("(c p) e -> p c e", p=P)).then_inc(gate_weight_in, 16)
            for dst, src in ((w_qk[:, :, :, :], wqk_t.rearrange("(c p) g f -> p c g f", p=P)),
                             (w_v[:, :, :], wv_t.rearrange("(c p) f -> p c f", p=P)),
                             (w_o[:, :, :], wo_t.rearrange("(c p) f -> p c f", p=P)),
                             (qk_bias[:, :], bqk.rearrange("g p -> p g")),
                             (v_bias[:, :], bv.rearrange("(c p) -> p c", p=P)),
                             (bo_row[:, :, :], bo.rearrange("(t d) -> t d", t=1).partition_broadcast(P))):
                eng.dma_start(dst, src).then_inc(weights_in, 16)

            def gate_round(slot, chunk):
                odd = slot % 2
                if 0 in chunk:
                    wait(eng, gate_lg_full, chunk[0] - 1)
                    for j in range(2):
                        eng.wait_ge(gate_xt_full, chunk[0] * 2 + (j + 1))
                        nc.scalar.activation(gate_xt_of(chunk[0], odd)[:, :, 2 * j * P:2 * (j + 1) * P],
                                             pair_view(gate_bank[odd][j]), ACT.Copy).then_inc(gate_xt_taken, 1)
                if 1 in chunk:
                    eng.wait_ge(gate_lg_full, chunk[1] + 1)
                    wait(eng, gate_lt_full, chunk[1] - 1)
                    nc.scalar.activation(gate_lg[1 - odd], gate_bank[1 - odd][2][:, 0:P], ACT.Copy)\
                        .then_inc(gate_lg_taken, 1)
                if 2 in chunk:
                    eng.wait_ge(gate_lt_full, chunk[2] + 1)
                    nc.scalar.activation(logits[:, bass.ds(chunk[2] * CT, CT), :], logits_view(gate_bank[odd][3]),
                                         ACT.Copy).then_inc(gate_lt_taken, 1)

            gate_pipeline(eng, 3, gate_round)

            def moe_scalar(layer):
                def gate():
                    eng.wait_ge(baton[layer], 1)
                    _, work, left, _, _ = tables[layer]
                    nc.scalar.activation(work, left, ACT.Exp).then_inc(baton[layer], 1)

                def chunk(c, i, turn):
                    eng.wait_ge(baton[layer], turn(4))
                    for dc in range(DC):
                        dst = xg_t[:, dc, :] if i is c else x_t[:, dc, c * CW:(c + 1) * CW]
                        last = nc.scalar.activation(dst, st_bank[dc][:, :], ACT.Copy)
                    last.then_inc(baton[layer], 1)

                def expert(c, e):
                    eng.wait_ge(baton[layer], moe_value(c, e, 1))
                    for fc in range(DC):
                        nc.scalar.activation(hidden[:, fc, :], st_bank[fc][:, :], ACT.Identity,
                                             bias=b1_e[:, fc:fc + 1])
                    eng.drain()
                    nc.scalar.activation(hidden_e, hidden, ACT.Exp, scale=-1.0).then_inc(baton[layer], 1)

                moe_experts(eng, layer, gate, chunk, expert)

            def evict(b, n, hg, what, *a):
                if what in ("otr", "wo"):
                    return
                eng.wait_ge(misc_full, n("use", 1))
                if what == "v":
                    j = a[0]
                    nc.scalar.activation(v_aug[:, 2 * j:2 * j + 2, :, 0:HD],
                                         misc[:, :].rearrange("p (t h d) -> p t h d", t=2, d=HD), ACT.Copy)\
                        .then_inc(misc_free, 1)
                elif what == "qk":
                    hq, c = a
                    m = hq if hg == 0 else hq + NG
                    wait(eng, parts_out[c], lin(b, 32 * NG, 32 * m))
                    wait(eng, rest_ready, lin(b, 2 * NG, 2 * m + c))
                    for dst in (qk32[:, :], parts[:, c, 0, :]):
                        last = nc.scalar.activation(dst, misc[:, :], ACT.Identity, bias=qk_bias[:, hq:hq + 1],
                                                    scale=qk_scale[:, :])
                    last.then_inc(misc_free, 1)
                elif what == "xt":
                    c, j = a
                    t0 = c * CW + 2 * j * P
                    nc.scalar.activation(x_t[:, :, t0:t0 + 2 * P], pair_view(misc), ACT.Copy).then_inc(misc_free, 1)
                elif what == "xg":
                    j = a[1]
                    nc.scalar.activation(xg_t[:, :, 2 * j * P:2 * (j + 1) * P], pair_view(misc), ACT.Copy)\
                        .then_inc(misc_free, 1)
                elif what == "lg":
                    nc.scalar.activation(lg_t[:, :], misc[:, 0:P], ACT.Copy).then_inc(misc_free, 1)
                elif what == "lt":
                    nc.scalar.activation(logits[:, bass.ds(b * TB + (a[0] * CT + BATCH[a[1]] * TB), CT), :], logits_view(misc),
                                         ACT.Copy).then_inc(misc_free, 1)
                elif what == "ont":
                    for dc in range(DC):
                        last = nc.scalar.activation(o_t[:, dc, :], misc[:, dc * 2 * P:(dc + 1) * 2 * P],
                                                    ACT.Identity, bias=v_bias[:, dc:dc + 1])
                    last.then_inc(misc_free, 1)
                elif what == "mtr":
                    wait(eng, max_in[hg], lin(b, MAX_IN, MAX_IN))
                    nc.scalar.activation(max_t[:, :], misc16[0:HG * MROWS * TB, 0:P], ACT.Copy)\
                        .then_inc(misc_free, 1)

            def handle(b, n, hg, kind, *a):
                if kind == "st":
                    g, h = a
                    u = HG * g + h
                    off = group_shape(g)[2]
                    if h == 0:
                        wait(eng, pv_done, lin(b, NGRP * NG, NGRP * hg + g - 1))
                    eng.wait_ge(st_full, lin(b, NU * NG, NU * hg + u + 1))
                    nc.scalar.activation(probs[:, g % 2, h, 0:CW - off], st_bank[u % 3][:, 0:CW - off], ACT.Exp)\
                        .then_inc(exp_done, 1)
                elif kind == "oev":
                    c = a[0]
                    eng.wait_ge(pv_done, lin(b, NGRP * NG, NGRP * hg + (CT, 0)[c]))
                    nc.scalar.activation(o_raw[:, c * CW:(c + 1) * CW], o_bank[:, :], ACT.Copy).then_inc(o_out, 1)
                elif kind == "use":
                    evict(b, n, hg, *a)

            moe_scalar(0)
            eng.wait_ge(bias_scaled, 1)
            walk(eng, handle)
            moe_scalar(1)

        @block.vector
        def _(eng):
            for bank in st_bank + s_bank + [o_bank, misc]:
                nc.vector.memset(bank[:, :], 0.0)
            eng.drain().then_inc(consts_ready, 1)

            def gate_round(slot, chunk):
                odd = slot % 2
                if 0 in chunk:
                    c = chunk[0]
                    eng.wait_ge(x_in[slot], (c - slot) * (16 // LOADS) + 16)
                    wait(eng, stats_ready, c)
                    for t in range(CT):
                        vector_stats(t, c * CT + t)
                if 1 in chunk:
                    c = chunk[1]
                    eng.wait_ge(rstd_ready, c + 1)
                    wait(eng, gate_xt_full, c * 2 - 2)
                    for t in range(CT):
                        vector_normalise(t, c * CT + t, gate_xn[1 - odd]).then_inc(xn_ready, 1)
                if 0 in chunk:
                    vector_aggregate(eng).then_inc(stats_ready, 1)

            gate_pipeline(eng, 2, gate_round)

            def top2(layer, t0, t1):
                vec = nc.vector
                chosen, work, left, top, best = (table[:, t0:t1, :] for table in tables[layer])
                wide = lambda ap: ap.to_broadcast([P, t1 - t0, E])
                for choice, (of, to) in enumerate(((logits[:, t0:t1, :], chosen), (left, work))):
                    eng.drain()
                    vec.tensor_reduce(top[:, :, 0], of, AX.X, ALU.max)
                    eng.drain()
                    vec.tensor_tensor(work, of, wide(top), ALU.is_equal)
                    eng.drain()
                    vec.tensor_tensor(work, work, wide(rank[:, :, :]), ALU.mult)
                    eng.drain()
                    vec.tensor_reduce(best[:, :, 0], work, AX.X, ALU.max)
                    eng.drain()
                    vec.tensor_tensor(to, work, wide(best), ALU.is_equal)
                    eng.drain()
                    if choice == 0:
                        vec.scalar_tensor_tensor(out=left, in0=chosen, scalar=-BIG, in1=logits[:, t0:t1, :],
                                                 op0=ALU.mult, op1=ALU.add)
                    else:
                        vec.tensor_tensor(chosen, chosen, work, ALU.add)

            def count_and_decide(layer):
                vec, chosen = nc.vector, tables[layer][0]
                eng.drain()
                vec.tensor_reduce(counts[:, :], chosen.rearrange("p t e -> p e t"), AX.X, ALU.add)\
                    .then_inc(counted, 1)
                if layer == 0:
                    eng.wait_ge(weights_in, 16 * WEIGHT_DMAS)
                    nc.vector.tensor_scalar(qk_bias[0:HG * HD, :], qk_bias[0:HG * HD, :], HD ** -0.5, None,
                                            ALU.mult).then_inc(bias_scaled, 1)
                eng.wait_ge(totalled, layer + 1)
                vec.tensor_scalar(kept[:, 0, :], total[:, :], float(CAP), None, ALU.is_le)
                eng.drain()
                vec.tensor_reduce(any_kept[:, :], kept[:, 0, :], AX.X, ALU.max)
                eng.drain()
                vec.tensor_copy(flag[:, :], any_kept[:, :]).then_inc(flag_ready, 1)

            def moe_vector(layer):
                vec = nc.vector
                chosen, work, left, top, best = tables[layer]
                wide = lambda ap: ap.to_broadcast([P, NT, E])

                def gate():
                    vec.tensor_reduce(top[:, :, 0], logits[:, :, :], AX.X, ALU.max)
                    eng.drain()
                    vec.tensor_tensor(left, logits[:, :, :], wide(top), ALU.subtract)\
                        .then_inc(baton[layer], 1)
                    eng.wait_ge(baton[layer], 2)
                    vec.tensor_reduce(top[:, :, 0], work, AX.X, ALU.add)
                    eng.drain()
                    vec.reciprocal(best, top)
                    eng.drain()
                    vec.tensor_tensor(work, work, wide(best), ALU.mult)
                    eng.drain()
                    vec.tensor_tensor(work, work, chosen, ALU.mult)
                    eng.drain()
                    vec.tensor_tensor(work, work, wide(kept[:, :, :]), ALU.mult)
                    eng.drain()
                    vec.tensor_scalar(work, work, 0.5, None, ALU.mult).then_inc(baton[layer], 1)

                def chunk(c, i, turn):
                    eng.wait_ge(baton[layer], turn(0))
                    for t in range(CT):
                        vector_stats(t, c * CT + t)
                    vector_aggregate(eng).then_inc(baton[layer], 1)
                    eng.wait_ge(baton[layer], turn(2))
                    for t in range(CT):
                        last = vector_normalise(t, c * CT + t)
                    last.then_inc(baton[layer], 1)

                weight = work.rearrange("p t e -> p (t e)")

                def expert(c, e):
                    eng.wait_ge(baton[layer], moe_value(c, e, 2))
                    vec.tensor_scalar(hidden_e, hidden_e, 1.0, None, ALU.add)
                    eng.drain()
                    vec.reciprocal(hidden_e, hidden_e)
                    eng.drain()
                    vec.tensor_tensor(hidden, hidden, hidden_e, ALU.mult).then_inc(baton[layer], 1)
                    eng.wait_ge(baton[layer], moe_value(c, e, 4))
                    for j in range(2):
                        vec.tensor_tensor(y_e[:, 2 * j:2 * j + 2, :],
                                          s_bank[j][:, :].rearrange("p (t d) -> p t d", t=2),
                                          b2_e.to_broadcast([P, 2, D]), ALU.add)
                    eng.drain()
                    for t in range(CT):
                        tile = x_tiles(c * CT + t, 1)[:, 0, :]
                        last = vec.scalar_tensor_tensor(out=tile, in0=y_e[:, t, :],
                                                        scalar=weight[:, bass.ds(c * (CT * E) + e + t * E, 1)],
                                                        in1=tile, op0=ALU.mult, op1=ALU.add)
                    last.then_inc(baton[layer], 1)

                moe_experts(eng, layer, gate, chunk, expert)

            def handle(b, n, hg, kind, *a):
                if kind == "s":
                    ahead, u = a
                    ib, h, j0, width, diag = MAX_UNITS[u]
                    eng.wait_ge(s_full, lin(b, NU * NG, NU * (hg + ahead) + u + 1))
                    if diag:
                        passed(eng, "vector")
                    bank = s_bank[u % 3][:, 0:width]
                    if diag:
                        nc.vector.tensor_tensor_reduce(out=bank, in0=bank, in1=causal[:, CW - width:CW],
                                                       scale=1.0, scalar=-BIG, op0=ALU.add, op1=ALU.max,
                                                       accum_out=max_diag[:, (hg + ahead) % 2, h, ib:ib + 1]).then_inc(max_done, 1)
                    else:
                        nc.vector.tensor_reduce(max_full[:, (hg + ahead) % 2, h, ib - CT:ib - CT + 1], bank, AX.X, ALU.max)\
                            .then_inc(max_done, 1)
                elif kind == "mfin":
                    step = (hg + 1) % 2
                    mx, rest_of = max_diag[:, step, :, :], max_rest[:, :, :]
                    eng.drain()
                    if a[0] == 0:
                        late = max_diag[:, step, :, CT:TB]
                        nc.vector.tensor_tensor(late, late, max_full[:, step, :, :], ALU.max)
                    elif a[0] == 1:
                        nc.vector.tensor_scalar(max_parts[:, 0, :, :], mx, -1.0, None, ALU.mult)
                    elif a[0] == 2:
                        nc.vector.scalar_tensor_tensor(out=rest_of, in0=mx, scalar=-1.0,
                                                       in1=max_parts[:, 0, :, :], op0=ALU.mult, op1=ALU.subtract)
                    elif a[0] == 3:
                        nc.vector.tensor_copy(max_parts[:, 1, :, :], rest_of)
                    else:
                        nc.vector.tensor_tensor(max_parts[:, 2, :, :], rest_of, max_parts[:, 1, :, :],
                                                ALU.subtract).then_inc(mparts_ready, 1)
                elif kind in ("lnstat", "lnnorm"):
                    what, c, t = a
                    tile = lin(b, TB, BATCH[what] * TB + c * CT + t)
                    if kind == "lnstat":
                        if t == 0:
                            eng.drain()
                        vector_stats(t, tile)
                    else:
                        if t == 0:
                            eng.wait_ge(rstd_ready, n("lnaggr"))
                            eng.wait_ge(misc_full, n("use"))
                        vector_normalise(t, tile).then_inc(xn_ready, 1)
                elif kind == "lnaggr":
                    vector_aggregate(eng).then_inc(stats_ready, 1)
                elif kind == "top2":
                    eng.wait_ge(misc_free, n("use", 1))
                    top2(1, 0, TOP2_EARLY)
                elif kind == "q2":
                    hq, c = a
                    m = hq if hg == 0 else hq + NG
                    eng.wait_ge(rest_ready, lin(b, 2 * NG, 2 * m + c + 1))
                    nc.vector.tensor_copy(parts[:, c, 1, :], rest[:, :]).then_inc(part2_ready, 1)
                elif kind == "use" and a[0] == "otr":
                    hq, c = a[1:]
                    eng.wait_ge(misc_full, n("use", 1))
                    heads = misc[:, :].rearrange("p (q w) -> p q w", w=32)
                    nc.vector.reciprocal(sum_inv[:, :, :], heads[:, :, HD:VW])
                    eng.drain()
                    nc.vector.tensor_tensor(
                        o_tok[:, c * CT:(c + 1) * CT, hq * HG * HD:(hq + 1) * HG * HD]
                        .rearrange("p t (h d) -> p t h d", h=HG),
                        heads[:, :, 0:HD].rearrange("p (t h) d -> p t h d", t=CT),
                        sum_inv[:, :, :].to_broadcast([P, CT * HG, HD])
                        .rearrange("p (t h) d -> p t h d", t=CT), ALU.mult).then_inc(misc_free, 1)
                elif kind == "use" and a[0] == "wo":
                    j, what = a[1:]
                    eng.wait_ge(misc_full, n("use", 1))
                    eng.wait_ge(bo_added, lin(b, 4, j + 1 + BATCH[what] * 4))
                    now = x_tiles(b * TB + (2 * j + BATCH[what] * TB), 2)
                    nc.vector.tensor_tensor(now, misc[:, :].rearrange("p (t d) -> p t d", t=2), now, ALU.add)\
                        .then_inc(misc_free, 1)

            eng.wait_ge(gate_lt_taken, NCH)
            top2(0, 0, NT)
            count_and_decide(0)
            moe_vector(0)
            walk(eng, handle)
            eng.wait_ge(misc_free, COUNTS_AFTER["use"] + 1)
            top2(1, TOP2_EARLY, NT)
            count_and_decide(1)
            moe_vector(1)

        @block.tensor
        def _(eng):
            eng.wait_ge(consts_ready, CONSTS)
            eng.wait_ge(gate_weight_in, 16)
            def gate_round(slot, chunk):
                odd = slot % 2
                if 0 in chunk:
                    eng.wait_ge(xn_ready, chunk[0] * CT + CT)
                    for j in range(2):
                        wait(eng, gate_xt_taken, chunk[0] * 2 + (j - 3))
                        tensor_transpose_tiles(gate_bank[odd][j], gate_xn[odd], 2 * j).then_inc(gate_xt_full, 1)
                if 1 in chunk:
                    eng.wait_ge(gate_xt_taken, chunk[1] * 2 + 2)
                    wait(eng, gate_lg_taken, chunk[1] - 1)
                    tensor_gate_logits(gate_bank[1 - odd][2], gate_xt_of(chunk[1], 1 - odd)).then_inc(gate_lg_full, 1)
                if 2 in chunk:
                    eng.wait_ge(gate_lg_taken, chunk[2] + 1)
                    wait(eng, gate_lt_taken, chunk[2] - 1)
                    nc.tensor.transpose(gate_bank[odd][3][:, 0:P], gate_lg[odd], ident[:, :])\
                        .then_inc(gate_lt_full, 1)

            gate_pipeline(eng, 3, gate_round)

            def moe_tensor(layer):
                def chunk(c, i, turn):
                    eng.wait_ge(baton[layer], turn(3))
                    for t in range(CT):
                        for dc in range(DC):
                            last = nc.tensor.transpose(st_bank[dc][:, t * P:(t + 1) * P],
                                                       xn[:, t, dc * P:(dc + 1) * P], ident[:, :])
                    last.then_inc(baton[layer], 1)

                def expert(c, e):
                    eng.wait_ge(baton[layer], moe_value(c, e, 0))
                    eng.wait_ge(moe_weights_in[layer], c * (64 * E) + e * 64 + 64)
                    for fc in range(DC):
                        for dc in range(DC):
                            last = nc.tensor.matmul(st_bank[fc][:, :], w1_e[:, dc, fc * P:(fc + 1) * P],
                                                    xg_t[:, dc, :], start=dc == 0, stop=dc == DC - 1)
                    last.then_inc(baton[layer], 1)
                    eng.wait_ge(baton[layer], moe_value(c, e, 3))
                    for t in range(CT):
                        for fc in range(DC):
                            last = nc.tensor.matmul(s_bank[t // 2][:, t % 2 * D:(t % 2 + 1) * D],
                                                    hidden[:, fc, t * P:(t + 1) * P], w2_e[:, fc, :],
                                                    start=fc == 0, stop=fc == DC - 1)
                    last.then_inc(baton[layer], 1)

                moe_experts(eng, layer, None, chunk, expert)

            def fill(b, n, hg, what, *a):
                wait(eng, misc_free, n("use", 1))
                if what == "v":
                    for t in range(2):
                        for dc in range(DC):
                            t0 = (2 * a[0] + t) * P
                            last = nc.tensor.matmul(misc[:, t * D:(t + 1) * D], x_t[:, dc, t0:t0 + P],
                                                    w_v[:, dc, :], start=dc == 0, stop=dc == DC - 1)
                elif what == "qk":
                    hq, c = a
                    for dc in range(DC):
                        last = nc.tensor.matmul(misc[:, :], w_qk[:, dc, hq, :], x_t[:, dc, c * CW:(c + 1) * CW],
                                                start=dc == 0, stop=dc == DC - 1)
                elif what in ("xt", "xg"):
                    eng.wait_ge(xn_ready, n("lnnorm"))
                    last = tensor_transpose_tiles(misc, xn, 2 * a[1])
                elif what == "lg":
                    last = tensor_gate_logits(misc, xg_t)
                elif what == "lt":
                    last = nc.tensor.transpose(misc[:, 0:P], lg_t[:, :], ident[:, :])
                elif what == "otr":
                    hq, c = a
                    own = hq == hg
                    eng.wait_ge(o_out, lin(b, 2 * NG, 2 * (hg + own) + c - 1))
                    for t in range(CT):
                        t0 = c * CW + t * P
                        last = nc.tensor.transpose(misc[:, t * P:(t + 1) * P], o_raw[:, t0:t0 + P], ident[:, :])
                elif what == "ont":
                    last = tensor_transpose_tiles(misc, o_tok, 2 * a[0])
                elif what == "wo":
                    for t in range(2):
                        for dc in range(DC):
                            last = nc.tensor.matmul(misc[:, t * D:(t + 1) * D], o_t[:, dc, t * P:(t + 1) * P],
                                                    w_o[:, dc, :], start=dc == 0, stop=dc == DC - 1)
                elif what == "mtr":
                    eng.wait_ge(mparts_ready, lin(b, NG, hg + 2))
                    last = nc.tensor.transpose(misc16[0:HG * MROWS * TB, 0:P],
                                               max_parts[:, :, :, :].rearrange("p k h t -> p (k h t)"),
                                               ident16[:, :])
                last.then_inc(misc_full, 1)

            def handle(b, n, hg, kind, *a):
                if kind == "st":
                    g, h = a
                    qc, jb, off, _ = group_shape(g)
                    u = HG * g + h
                    if u == 0:
                        eng.wait_ge(stack_in[hg], lin(b, STACK_IN, STACK_IN))
                        eng.wait_ge(max_in[hg], lin(b, MAX_IN, MAX_IN))
                    wait(eng, exp_done, lin(b, NU * NG, NU * hg + u - 2))
                    nc.tensor.matmul(st_bank[u % 3][:, 0:CW - off],
                                     k_stack[0:KROWS + MROWS, hg, h, jb * P:(jb + 1) * P],
                                     q_stack[0:KROWS + MROWS, hg, h, qc * CW + off:(qc + 1) * CW],
                                     start=True, stop=True).then_inc(st_full, 1)
                elif kind == "s":
                    ahead, u = a
                    hm = (hg + ahead) % NG
                    ib, h, j0, width, _ = MAX_UNITS[u]
                    if u == 0:
                        eng.wait_ge(stack_in[hm], lin(b, STACK_IN, STACK_IN * (1 + (hg + ahead) // NG)))
                    wait(eng, max_done, lin(b, NU * NG, NU * (hg + ahead) + u - 2))
                    nc.tensor.matmul(s_bank[u % 3][:, 0:width], q_stack[0:KROWS, hm, h, ib * P:(ib + 1) * P],
                                     k_stack[0:KROWS, hm, h, j0:j0 + width], start=True, stop=True)\
                        .then_inc(s_full, 1)
                elif kind == "pv":
                    g = a[0]
                    back = g >= NGRP - 2
                    of = hg - back
                    _, jb, off, diag = group_shape(g)
                    if g == 0:
                        wait(eng, o_out, lin(b, 2 * NG, 2 * hg))
                    if g == CT:
                        eng.wait_ge(o_out, lin(b, 2 * NG, 2 * hg + 1))
                    if hg == 0 and not back and jb % 2 == 0 and diag:
                        eng.wait_ge(misc_free, n("use", 1))
                    if diag:
                        eng.wait_ge(sel_done, lin(b, 8 * NG, 8 * of + (g if g < CT else g - CT) + 1))
                    else:
                        eng.wait_ge(exp_done, lin(b, NU * NG, NU * of + HG * g + HG))
                    for h in range(HG):
                        last = nc.tensor.matmul(o_bank[32 * h:32 * h + VW, off:CW],
                                                v_aug[:, jb, of % NG * HG + h, :],
                                                probs[:, g % 2, h, 0:CW - off], start=g in (0, CT),
                                                stop=g in (CT - 1, NGRP - 1))
                    last.then_inc(pv_done, 1)
                elif kind == "use":
                    fill(b, n, hg, *a)

            moe_tensor(0)
            eng.wait_ge(weights_in, 16 * WEIGHT_DMAS)
            walk(eng, handle)
            moe_tensor(1)


_OUT_SHAPE = (NT, P, D)


def kernel(L0_attn_x, L0_attn_Wq, L0_attn_bq, L0_attn_Wkv, L0_attn_bkv, L0_attn_Wo, L0_attn_bo,
           L0_ffn_gate_w, L0_ffn_w1, L0_ffn_b1, L0_ffn_w2, L0_ffn_b2):
    import numpy as np
    import concourse.bacc as bacc
    from concourse.bass_utils import run_bass_kernel_spmd

    def grouped(q, k):
        parts = [p.reshape(p.shape[:-1] + (NG, HG, HD)).swapaxes(-1, -2).reshape(p.shape[:-1] + (NG, HG * HD))
                 for p in (q, k)]
        return np.concatenate(parts, axis=-1)

    a = {n: np.asarray(v) for n, v in locals().items() if n.startswith("L0_")}
    wk, wv = a["L0_attn_Wkv"][:D], a["L0_attn_Wkv"][D:]
    arrays = {
        "x": a["L0_attn_x"].reshape(_OUT_SHAPE),
        "wqk_t": grouped(a["L0_attn_Wq"].T, wk.T),
        "wv_t": wv.T,
        "wo_t": a["L0_attn_Wo"].T,
        "bqk": grouped(a["L0_attn_bq"], a["L0_attn_bkv"][:D]),
        "bv": a["L0_attn_bkv"][D:],
        "bo": a["L0_attn_bo"],
        "gate_t": a["L0_ffn_gate_w"].T,
        "w1_t": a["L0_ffn_w1"].transpose(0, 2, 1),
        "b1": a["L0_ffn_b1"],
        "w2_t": a["L0_ffn_w2"].transpose(0, 2, 1),
        "b2": a["L0_ffn_b2"],
    }
    arrays = {n: np.ascontiguousarray(v) for n, v in arrays.items()}
    nc = bacc.Bacc("TRN2", target_bir_lowering=False, num_devices=1)
    nc.disable_value_cache = True
    args = [nc.dram_tensor(n, v.shape, mybir.dt.from_np(v.dtype), kind="ExternalInput").ap()
            for n, v in arrays.items()]
    out = nc.dram_tensor("out", _OUT_SHAPE, FP32, kind="ExternalOutput").ap()
    program(nc, *args, out)
    r = run_bass_kernel_spmd(nc, [arrays], core_ids=[0])
    return r.results[0]["out"].reshape(B, S, D)
```
